# Optimizing a Trainium2 kernel written in Bass

```python
import numpy as np
import jax
import jax.numpy as jnp

def _softmax(x, axis=-1):
    return jax.nn.softmax(x, axis=axis)

def _gelu(x):
    return jax.nn.gelu(x, approximate=True)

def _silu(x):
    return jax.nn.silu(x)

def _sigmoid(x):
    return jax.nn.sigmoid(x)

def _layernorm(x, axis=-1, eps=1e-05):
    m = jnp.mean(x, axis=axis, keepdims=True)
    v = jnp.var(x, axis=axis, keepdims=True)
    return (x - m) / jnp.sqrt(v + eps)

def _scatter_add(tgt, idx, src, axis=0):
    return tgt.at[idx].add(src)

def _segment_sum(src, seg, n):
    return jax.ops.segment_sum(src, seg, n)
kernel_name = 'mk_adaln_d1_jaxref_r8_3658cc'

def setup_inputs(seed: int=0):
    np.random.seed(seed)
    _w = jnp.asarray

    def _L0_attn_setup():
        import jax, jax.numpy as jnp
        import numpy as np
        N_HEAD = 16
        EPS = 1e-06

        def _linear_attention(q, k, v):
            B, H, D = (q.shape[1], q.shape[2], q.shape[3])

            def step(carry, qkv_t):
                S, z = carry
                qt, kt, vt = qkv_t
                S = S + kt[..., :, None] * vt[..., None, :]
                z = z + kt
                num = jnp.einsum('bhi,bhij->bhj', qt, S)
                den = jnp.sum(qt * z, axis=-1, keepdims=True)
                return ((S, z), num / (den + EPS))
            S0 = jnp.zeros((B, H, D, D), q.dtype)
            z0 = jnp.zeros((B, H, D), q.dtype)
            _, y = jax.lax.scan(step, (S0, z0), (q, k, v))
            return y
        key = jax.random.key(seed)
        k1, k2, k3 = jax.random.split(key, 3)
        B, T, C = (2, 256, 128)
        x = jax.random.normal(k1, (B, T, C), dtype=jnp.float32)
        w_attn = jax.random.normal(k2, (C, 3 * C), dtype=jnp.float32) * 0.02
        w_proj = jax.random.normal(k3, (C, C), dtype=jnp.float32) * 0.02
        return {'x': x, 'w_attn': w_attn, 'w_proj': w_proj}
    _L0_attn_in = _L0_attn_setup()

    def _L0_ffn_setup():
        import jax, jax.numpy as jnp
        import numpy as np
        D = 128
        H = 512
        E = 8
        B, N = (2, 256)
        key = jax.random.key(seed)
        ks = jax.random.split(key, 5)
        x = jax.random.normal(ks[0], (B, N, D), dtype=jnp.float32)
        W1 = jax.random.normal(ks[1], (E, D, H), dtype=jnp.float32) / np.sqrt(D)
        W2 = jax.random.normal(ks[2], (E, H, D), dtype=jnp.float32) / np.sqrt(H)
        Wg = jax.random.normal(ks[3], (D, E), dtype=jnp.float32) / np.sqrt(D)
        bg = jax.random.normal(ks[4], (E,), dtype=jnp.float32) * 0.01
        return {'x': x, 'W1': W1, 'W2': W2, 'Wg': Wg, 'bg': bg}
    _L0_ffn_in = _L0_ffn_setup()
    _L0_c = _w((lambda *s: np.random.randn(*s).astype(np.float32) * 0.05)(2, 128))
    _L0_wmod = _w((lambda *s: np.random.randn(*s).astype(np.float32) * 0.05)(128, 6 * 128) * 128 ** (-0.5))
    _d = {'L0_attn_x': _L0_attn_in['x'], 'L0_attn_w_attn': _L0_attn_in['w_attn'], 'L0_attn_w_proj': _L0_attn_in['w_proj'], 'L0_ffn_W1': _L0_ffn_in['W1'], 'L0_ffn_W2': _L0_ffn_in['W2'], 'L0_ffn_Wg': _L0_ffn_in['Wg'], 'L0_ffn_bg': _L0_ffn_in['bg'], 'L0_c': _L0_c, 'L0_wmod': _L0_wmod}
    _x0 = _d['L0_attn_x']
    _d['L0_attn_x'] = jax.random.normal(jax.random.fold_in(jax.random.key(seed), 1), (2, 2048, 128), dtype=_x0.dtype)
    del _x0
    return _d

def reference(L0_attn_x, L0_attn_w_attn, L0_attn_w_proj, L0_ffn_W1, L0_ffn_W2, L0_ffn_Wg, L0_ffn_bg, L0_c, L0_wmod):

    def _L0_attn_ref(x, w_attn, w_proj):
        import jax, jax.numpy as jnp
        import numpy as np
        N_HEAD = 16
        EPS = 1e-06

        def _linear_attention(q, k, v):
            B, H, D = (q.shape[1], q.shape[2], q.shape[3])

            def step(carry, qkv_t):
                S, z = carry
                qt, kt, vt = qkv_t
                S = S + kt[..., :, None] * vt[..., None, :]
                z = z + kt
                num = jnp.einsum('bhi,bhij->bhj', qt, S)
                den = jnp.sum(qt * z, axis=-1, keepdims=True)
                return ((S, z), num / (den + EPS))
            S0 = jnp.zeros((B, H, D, D), q.dtype)
            z0 = jnp.zeros((B, H, D), q.dtype)
            _, y = jax.lax.scan(step, (S0, z0), (q, k, v))
            return y
        B, T, C = x.shape
        H = N_HEAD
        D = C // H
        qkv = x @ w_attn
        q, k, v = jnp.split(qkv, 3, axis=-1)

        def to_tbhd(a):
            return a.reshape(B, T, H, D).transpose(1, 0, 2, 3)
        q = jax.nn.elu(to_tbhd(q)) + 1.0
        k = jax.nn.elu(to_tbhd(k)) + 1.0
        v = to_tbhd(v)
        y = _linear_attention(q, k, v)
        y = y.transpose(1, 0, 2, 3).reshape(B, T, C)
        return y @ w_proj

    def _L0_ffn_ref(x, W1, W2, Wg, bg):
        import jax, jax.numpy as jnp
        import numpy as np
        D = 128
        H = 512
        E = 8
        B, N = (2, 256)
        b, n, d = x.shape
        e = Wg.shape[1]
        xf = x.reshape(b * n, d)
        logits = xf @ Wg + bg
        one_hot = jax.nn.one_hot(jnp.argmax(logits, axis=-1), e, dtype=x.dtype)
        h = jax.nn.gelu(jnp.einsum('td,edh->eth', xf, W1), approximate=True)
        y = jnp.einsum('eth,ehd->etd', h, W2)
        out = jnp.einsum('etd,te->td', y, one_hot)
        return out.reshape(b, n, d)
    x = L0_attn_x
    mod = (_silu(L0_c) @ L0_wmod).reshape(L0_c.shape[0], 6, 1, -1)
    sa, ca, ga, sb, cb, gb = (mod[:, 0], mod[:, 1], mod[:, 2], mod[:, 3], mod[:, 4], mod[:, 5])
    ga = (2 * (ga >= 0) - 1) * jnp.maximum(jnp.abs(ga), 0.25)
    gb = (2 * (gb >= 0) - 1) * jnp.maximum(jnp.abs(gb), 0.25)
    h = _layernorm(x, axis=-1) * (1 + ca) + sa
    x = x + ga * _L0_attn_ref(h, L0_attn_w_attn, L0_attn_w_proj)
    h = _layernorm(x, axis=-1) * (1 + cb) + sb
    x = x + gb * _L0_ffn_ref(h, L0_ffn_W1, L0_ffn_W2, L0_ffn_Wg, L0_ffn_bg)
    return x

_drawn_inputs = setup_inputs


def setup_inputs(seed=0):
    import zlib

    import numpy as np

    out = dict(_drawn_inputs(seed))
    spreads = {}
    factors = {'L0_attn_w_attn': 8.0, 'L0_attn_w_proj': 8.0, 'L0_ffn_bg': 3.051}
    for name, (base, spread) in spreads.items():
        noise = np.random.default_rng([zlib.crc32(name.encode()), seed]).standard_normal(out[name].shape)
        drawn = base * np.exp(spread * noise) if base else spread * noise
        out[name] = jnp.asarray(drawn.astype(out[name].dtype))
    for name, factor in factors.items():
        out[name] = (out[name] * factor).astype(out[name].dtype)
    return out
```

```python
from contextlib import ExitStack

import concourse.bass as bass
from concourse import mybir

F32 = mybir.dt.float32
I32 = mybir.dt.int32
ALU = mybir.AluOpType
ACT = mybir.ActivationFunctionType
AX = mybir.AxisListType

B, T, C = 2, 2048, 128
HEADS, HD = 16, 8
E, HID = 8, 512
P = 128
NT = B * T // P
GT = 4
G = NT // GT
L = 64
HC = HID // P
SLOT_TILES = NT + E
QUADS = 4
EPS = 1e-5
DEN_EPS = 1e-6
MOD_MIN = 0.25


class Count:

    def __init__(self, eng, sem, before=0):
        self.eng, self.sem, self.before, self.n = eng, sem, before, 0

    def link(self, ins):
        self.n += 1
        ins.then_inc(self.sem, 1)
        self.eng.wait_ge(self.sem, self.before + self.n)


def build(nc, x, w_attn, w_proj, w1, w2, wg, bg, c, wmod, out):
    sorted_h = nc.dram_tensor("sorted_h", (SLOT_TILES * P, C), F32, kind="Internal").ap()
    sorted_y = nc.dram_tensor("sorted_y", (SLOT_TILES * P, C), F32, kind="Internal").ap()

    with ExitStack() as ctx:
        def sb(name, shape, dt=F32):
            return ctx.enter_context(nc.sbuf_tensor(name, shape, dt))

        def sem(name):
            return ctx.enter_context(nc.semaphore(name))

        x_all = sb("x_all", [P, NT, C])
        h2_all = sb("h2_all", [P, NT, C])
        w1_all = sb("w1_all", [P, E, HID])
        w2_all = sb("w2_all", [P, E, HC, C])
        wqkv = sb("wqkv", [P, 3 * C])
        wproj = sb("wproj", [P, C])
        wproj_b = sb("wproj_b", [P, B, C])
        wg_sb = sb("wg_sb", [P, E])
        bg_row = sb("bg_row", [1, E])
        bg_bc = sb("bg_bc", [P, E])
        wmod_sb = sb("wmod_sb", [P, 6 * C])
        c_col = sb("c_col", [P, B])
        c_exp = sb("c_exp", [P, B])
        c_silu = sb("c_silu", [P, B])
        c_bc = sb("c_bc", [P, B, P])
        sa_col = sb("sa_col", [P, B])
        ca1_col = sb("ca1_col", [P, B])
        mod_bc = sb("mod_bc", [P, B, 4, C])
        gate_a = sb("gate_a", [P, B, 2, C])
        gate_s = sb("gate_s", [P, B, 2, C])
        ident = sb("ident", [P, P])
        ones = sb("ones", [P, P])
        zeros = sb("zeros", [P, 2 * P])
        upper = sb("upper", [P, P])
        block = sb("block", [P, P])
        quad_head = sb("quad_head", [P, QUADS])
        causal = sb("causal", [P, QUADS, L])
        iota_tok = sb("iota_tok", [P, E, NT])
        iota_tile = sb("iota_tile", [1, SLOT_TILES, E])
        prefer = sb("prefer", [P, NT, E])
        stats = [sb(f"stats{n}", [P, NT, 6]) for n in range(2)]
        mean = [sb(f"mean{n}", [P, NT]) for n in range(2)]
        var = sb("var", [P, NT])
        diff = sb("diff", [P, NT])
        root = sb("root", [P, NT])
        rstd = [sb(f"rstd{n}", [P, NT]) for n in range(2)]
        xhat = sb("xhat", [P, GT, C])
        h_t = sb("h_t", [P, GT * P])
        relu_q = sb("relu_q", [P, GT * P])
        relu_k = sb("relu_k", [P, GT * P])
        exp_q = sb("exp_q", [P, GT * P])
        exp_k = sb("exp_k", [P, GT * P])
        q_t = [sb(f"q_t{n}", [P, GT * P]) for n in range(2)]
        k_t = [sb(f"k_t{n}", [P, GT * P]) for n in range(2)]
        q_m = [sb(f"q_m{n}", [P, 2 * GT, QUADS, L]) for n in range(2)]
        k_n = [sb(f"k_n{n}", [P, GT, C]) for n in range(2)]
        v_n = [sb(f"v_n{n}", [P, GT, C]) for n in range(2)]
        v_m = [sb(f"v_m{n}", [P, GT, QUADS * (P + HD)]) for n in range(2)]
        z_t = [sb(f"z_t{n}", [P, GT * P]) for n in range(2)]
        qz = sb("qz", [P, GT * P])
        den = sb("den", [P, GT * P])
        rden = [sb(f"rden{n}", [P, GT * P]) for n in range(2)]
        probs = sb("probs", [P, B, QUADS, QUADS * L])
        state = sb("state", [P, 2, B, C])
        y_n = sb("y_n", [P, 2, B, P])
        h2_s = [sb(f"h2_s{n}", [P, GT, C]) for n in range(2)]
        h2_t = [sb(f"h2_t{n}", [P, GT * P]) for n in range(2)]
        logit = sb("logit", [P, NT, E])
        best = sb("best", [P, NT])
        onehot = sb("onehot", [P, NT, E])
        tot = sb("tot", [P, E, NT])
        cum = sb("cum", [P, E, NT])
        cnt = sb("cnt", [P, E])
        r_cmp = sb("r_cmp", [P, E, NT])
        tiles_e = sb("tiles_e", [P, E])
        tiles_cum = sb("tiles_cum", [P, E])
        base_e = sb("base_e", [P, E])
        slot_f = sb("slot_f", [P, NT])
        slot_i = sb("slot_i", [P, NT], I32)
        t_cmp = sb("t_cmp", [1, SLOT_TILES, E])
        t_exp = sb("t_exp", [1, SLOT_TILES])
        t_expert = sb("t_expert", [1, SLOT_TILES], I32)
        h_row = [sb(f"h_row{n}", [P, C]) for n in range(2)]
        h_col = [sb(f"h_col{n}", [P, P]) for n in range(2)]
        w1_cur = [sb(f"w1_cur{n}", [P, HID]) for n in range(2)]
        w2_cur = [sb(f"w2_cur{n}", [P, HC, C]) for n in range(2)]
        gelu = [sb(f"gelu{n}", [P, HC, P]) for n in range(2)]
        y_row = [sb(f"y_row{n}", [P, C]) for n in range(2)]

        bank = [ctx.enter_context(nc.psum_tensor(f"bank{n}", [P, 512], F32)) for n in range(8)]
        F0, F1, F2, S0, S1, ST, Y0, Y1 = bank
        score_bank, y_bank = [S0, S1], [Y0, Y1]

        x_in = [sem(f"x_in{g}") for g in range(G)]
        c_in, wmod_in, wqkv_in, wproj_in, wgate_in, w1_in, w2_in = (
            sem(n) for n in ("c_in", "wmod_in", "wqkv_in", "wproj_in", "wgate_in", "w1_in", "w2_in"))
        consts, masks = sem("consts"), sem("masks")
        c_exp_done, c_ready, mod_mm, mod_ready = (sem(n) for n in ("c_exp_done", "c_ready", "mod_mm", "mod_ready"))
        var_ready, root_ready = sem("var_ready"), sem("root_ready")
        dve_chain, act_chain, pool_chain = sem("dve_chain"), sem("act_chain"), sem("pool_chain")
        xhat_ready, xt_mm, ht_ready = sem("xhat_ready"), sem("xt_mm"), sem("ht_ready")
        q_mm, k_mm, v_mm, kt_mm, den_mm = (sem(n) for n in ("q_mm", "k_mm", "v_mm", "kt_mm", "den_mm"))
        eq_ready, ek_ready, q_ready, k_ready, qm_ready = (
            sem(n) for n in ("eq_ready", "ek_ready", "q_ready", "k_ready", "qm_ready"))
        v_ready, kn_ready, qz_ready, rden_ready = (sem(n) for n in ("v_ready", "kn_ready", "qz_ready", "rden_ready"))
        score_mm, probs_ready = sem("score_mm"), sem("probs_ready")
        kv_mm, state_ready, y_mm, y_ready = (sem(n) for n in ("kv_mm", "state_ready", "y_mm", "y_ready"))
        proj_mm, x1_ready = sem("proj_mm"), sem("x1_ready")
        h2_ready, h2t_mm, h2t_ready, h2_kept, logit_mm = (
            sem(n) for n in ("h2_ready", "h2t_mm", "h2t_ready", "h2_kept", "logit_mm"))
        onehot_ready, rank_mm, slots_ready, zeroed, scattered = (
            sem(n) for n in ("onehot_ready", "rank_mm", "slots_ready", "zeroed", "scattered"))
        row_in = [sem(f"row_in{n}") for n in range(2)]
        row_mm, col_ready, w1c_ready, w2c_ready, up_mm, gelu_ready, down_mm, yrow_ready = (
            sem(n) for n in ("row_mm", "col_ready", "w1c_ready", "w2c_ready", "up_mm", "gelu_ready", "down_mm",
                             "yrow_ready"))
        row_out = [sem(f"row_out{n}") for n in range(2)]
        gathered = [sem(f"gathered{g}") for g in range(G)]
        out_ready, stored = sem("out_ready"), sem("stored")

        x_v = x.rearrange("b (g s p) c -> b g p s c", s=2, p=P)
        out_v = out.rearrange("b (g s p) c -> b g p s c", s=2, p=P)
        sorted_h_v = sorted_h.rearrange("(n p) c -> n p c", p=P)
        sorted_y_v = sorted_y.rearrange("(n p) c -> n p c", p=P)

        blk = ctx.enter_context(nc.Block())

        @blk.sync
        def _(sp):
            with nc.allow_non_contiguous_dma(reason="256 values of c, by column"):
                sp.dma_start(c_col[:], c.rearrange("b c -> c b")).then_inc(c_in, 16)
            sp.dma_start(wmod_sb[:], wmod).then_inc(wmod_in, 16)
            for g in range(G):
                for b in range(B):
                    sp.dma_start(x_all[:, GT * g + 2 * b:GT * g + 2 * b + 2, :], x_v[b, g]).then_inc(x_in[g], 16)
            sp.dma_start(w1_all[:], w1.rearrange("e d h -> d e h")).then_inc(w1_in, 16)
            sp.dma_start(w2_all[:], w2.rearrange("e (k p) d -> p e k d", p=P)).then_inc(w2_in, 16)

            sp.wait_ge(scattered, 16 * NT)

            def load(n, n_par, k):
                sp.wait_ge(row_mm, n - 1) if not isinstance(n, int) or n >= 2 else None
                sp.dma_start(h_row[n_par][:], sorted_h_v[bass.ds(n, 1)].rearrange("o p c -> p (o c)")
                             if not isinstance(n, int) else sorted_h_v[n]).then_inc(row_in[n_par], 16)

            def store(n, n_par):
                sp.wait_ge(yrow_ready, n + 1)
                sp.dma_start(sorted_y_v[bass.ds(n, 1)].rearrange("o p c -> p (o c)")
                             if not isinstance(n, int) else sorted_y_v[n], y_row[n_par][:]).then_inc(row_out[n_par], 16)

            load(0, 0, 0)
            load(1, 1, 0)
            with sp.Fori(0, SLOT_TILES // 2 - 1) as k:
                for par in range(2):
                    load(2 * k + 2 + par, par, k + 1)
                    store(2 * k + par, par)
            for par in range(2):
                store(SLOT_TILES - 2 + par, par)

            for g in range(G):
                sp.wait_ge(out_ready, g + 1)
                for b in range(B):
                    sp.dma_start(out_v[b, g], x_all[:, GT * g + 2 * b:GT * g + 2 * b + 2, :]).then_inc(stored, 16)
            sp.wait_ge(stored, 16 * G * B)

        @blk.gpsimd
        def _(pool):
            chain = Count(pool, pool_chain)
            chain.link(nc.gpsimd.memset(zeros[:], 0.0))
            chain.link(nc.gpsimd.memset(ident[:], 0.0))
            nc.gpsimd.affine_select(out=ident[:], in_=ident[:], compare_op=ALU.not_equal, fill=1.0, base=0,
                                    pattern=[[-1, P]], channel_multiplier=1).then_inc(consts, 1)
            chain.link(nc.gpsimd.memset(ones[:], 1.0))
            nc.gpsimd.affine_select(out=upper[:], in_=ones[:], compare_op=ALU.is_gt, fill=0.0, base=0,
                                    pattern=[[1, P]], channel_multiplier=-1).then_inc(consts, 1)
            bl = block[:].rearrange("p (h j) -> p h j", j=HD)
            chain.link(nc.gpsimd.affine_select(out=bl, in_=ones[:].rearrange("p (h j) -> p h j", j=HD),
                                               compare_op=ALU.is_ge, fill=0.0, base=0,
                                               pattern=[[-HD, HEADS], [0, HD]], channel_multiplier=1))
            nc.gpsimd.affine_select(out=bl, in_=bl, compare_op=ALU.is_ge, fill=0.0, base=HD - 1,
                                    pattern=[[HD, HEADS], [0, HD]], channel_multiplier=-1).then_inc(masks, 1)
            chain.link(nc.gpsimd.memset(causal[:], 1.0))
            for half in range(2):
                rows = slice(L * half, L * half + L)
                nc.gpsimd.affine_select(out=causal[rows], in_=causal[rows], compare_op=ALU.is_ge, fill=0.0, base=0,
                                        pattern=[[0, QUADS], [1, L]], channel_multiplier=-1).then_inc(masks, 1)
                pool.wait_ge(masks, 2 + half)
            for n in range(2):
                nc.gpsimd.memset(v_m[n][:], 0.0).then_inc(masks, 1)
            nc.gpsimd.iota(iota_tok[:], pattern=[[0, E], [P, NT]], base=0, channel_multiplier=0,
                           allow_small_or_imprecise_dtypes=True).then_inc(masks, 1)
            nc.gpsimd.iota(iota_tile[:], pattern=[[1, SLOT_TILES], [0, E]], base=0, channel_multiplier=0,
                           allow_small_or_imprecise_dtypes=True).then_inc(masks, 1)
            nc.gpsimd.iota(prefer[:], pattern=[[0, NT], [-1, E]], base=E, channel_multiplier=0,
                           allow_small_or_imprecise_dtypes=True).then_inc(masks, 1)

            def masked_q(f, par):
                there = f + 1 if isinstance(f, int) else pool.to_reg(f + 1)
                pool.wait_ge(mod_ready, 1)
                pool.wait_ge(q_ready, there)
                for a in range(QUADS):
                    last = nc.gpsimd.tensor_scalar(q_m[par][:, :, a, :], q_t[par][:].rearrange("p (n t) -> p n t", t=L),
                                                   quad_head[:, a:a + 1], None, ALU.mult)
                last.then_inc(qm_ready, 1)

            masked_q(0, 0)
            with pool.Fori(0, G // 2 - 1) as k:
                masked_q(2 * k + 1, 1)
                masked_q(2 * k + 2, 0)
            masked_q(G - 1, 1)

            pool.wait_ge(slots_ready, 1)
            pool.wait_ge(zeroed, 16)
            pool.wait_ge(h2_kept, G)
            for n in range(NT):
                pool.indirect_dma_start(sorted_h, bass.IndirectOffsetOnAxis(ap=slot_i[:, n:n + 1], axis=0),
                                        h2_all[:, n, :], None).then_inc(scattered, 16)

            pool.wait_ge(w2_in, 16)

            def pick_w2(n, par, first=False):
                e = pool.value_load(t_expert[0:1, bass.ds(n, 1)], min_val=0, max_val=E - 1)
                if not first:
                    pool.wait_ge(down_mm, n - 1)
                nc.gpsimd.tensor_copy(w2_cur[par][:], w2_all[:, bass.ds(e, 1)].rearrange("p o k c -> p (o k) c")
                                      ).then_inc(w2c_ready, 1)

            pick_w2(0, 0, True)
            pick_w2(1, 1, True)
            with pool.Fori(1, SLOT_TILES // 2) as k:
                for par in range(2):
                    pick_w2(2 * k + par, par)

            for par in range(2):
                pool.wait_ge(row_out[par], 16 * (SLOT_TILES // 2))
            for n in range(NT):
                pool.indirect_dma_start(h2_all[:, n, :], None, sorted_y,
                                        bass.IndirectOffsetOnAxis(ap=slot_i[:, n:n + 1], axis=0)
                                        ).then_inc(gathered[n // GT], 16)

        @blk.scalar
        def _(act):
            act.dma_start(wqkv[:], w_attn).then_inc(wqkv_in, 16)
            act.dma_start(wproj[:], w_proj).then_inc(wproj_in, 16)
            act.dma_start(wg_sb[:], wg).then_inc(wgate_in, 16)
            act.dma_start(bg_row[:], bg.rearrange("(o e) -> o e", o=1)).then_inc(wgate_in, 16)
            chain = Count(act, act_chain)
            act.wait_ge(c_in, 16)
            nc.scalar.activation(c_exp[:], c_col[:], ACT.Exp, scale=-1.0).then_inc(c_exp_done, 1)
            act.wait_ge(pool_chain, 1)
            act.dma_start(sorted_h.rearrange("(n p) c -> p n c", p=P),
                          zeros[:, 0:C].unsqueeze(1).broadcast_to([P, SLOT_TILES, C])).then_inc(zeroed, 16)
            act.wait_ge(var_ready, 1)
            nc.scalar.activation(root[:], var[:], ACT.Sqrt).then_inc(root_ready, 1)
            act.wait_ge(mod_ready, 1)
            act.wait_ge(masks, 5)

            def front(f, par, chain):
                act.wait_ge(xt_mm, f + 1)
                for b in range(B):
                    cols = slice(2 * P * b, 2 * P * b + 2 * P)
                    last = nc.scalar.activation(h_t[:, cols], F0[:, cols], ACT.Identity, bias=sa_col[:, b:b + 1],
                                                scale=ca1_col[:, b:b + 1])
                last.then_inc(ht_ready, 1)
                act.wait_ge(q_mm, f + 1)
                chain.link(nc.scalar.activation(relu_q[:], F1[:], ACT.Relu, scale=-1.0))
                act.wait_ge(q_ready, f)
                nc.scalar.activation(exp_q[:], relu_q[:], ACT.Exp, scale=-1.0).then_inc(eq_ready, 1)
                act.wait_ge(k_mm, f + 1)
                chain.link(nc.scalar.activation(relu_k[:], F2[:], ACT.Relu, scale=-1.0))
                act.wait_ge(k_ready, f)
                nc.scalar.activation(exp_k[:], relu_k[:], ACT.Exp, scale=-1.0).then_inc(ek_ready, 1)
                act.wait_ge(v_mm, f + 1)
                nc.scalar.activation(v_n[par][:], F0[:], ACT.Copy)
                for t in range(GT):
                    diag = v_m[par][:, t].rearrange("p (a w) -> p a w", w=P + HD)[:, :, 0:P].rearrange(
                        "p a (q r) -> p a q r", q=QUADS)[:, :, :, 0:HD]
                    last = nc.scalar.activation(diag, F0[:, t * P:(t + 1) * P].rearrange(
                        "p (q a j) -> p a q j", q=QUADS, a=QUADS), ACT.Copy)
                last.then_inc(v_ready, 1)
                act.wait_ge(kt_mm, f + 1)
                nc.scalar.activation(k_n[par][:], F1[:], ACT.Copy).then_inc(kn_ready, 1)

            front(0, 0, chain)
            before = chain.n
            with act.Fori(0, G // 2 - 1) as k:
                front(2 * k + 1, 1, Count(act, act_chain, before + 4 * k))
                front(2 * k + 2, 0, Count(act, act_chain, before + 4 * k + 2))
            front(G - 1, 1, Count(act, act_chain, before + 4 * (G // 2 - 1)))

            act.wait_ge(var_ready, 2)
            nc.scalar.activation(root[:], var[:], ACT.Sqrt).then_inc(root_ready, 1)

            def gate(g, par):
                act.wait_ge(h2_ready, g + 1)
                nc.scalar.activation(h2_all[:, bass.ds(GT * g, GT), :], h2_s[par][:], ACT.Copy).then_inc(h2_kept, 1)
                act.wait_ge(h2t_mm, g + 1)
                nc.scalar.activation(h2_t[par][:], [F0, F1][par][:], ACT.Copy).then_inc(h2t_ready, 1)

            with act.Fori(0, G // 2) as k:
                gate(2 * k, 0)
                gate(2 * k + 1, 1)

            def experts(n, par):
                act.wait_ge(up_mm, n + 1)
                nc.scalar.activation(gelu[par][:], [S0, S1][par][:], ACT.Gelu_apprx_tanh).then_inc(gelu_ready, 1)

            with act.Fori(0, SLOT_TILES // 2) as k:
                experts(2 * k, 0)
                experts(2 * k + 1, 1)

        @blk.vector
        def _(dve):
            V = nc.vector
            chain = Count(dve, dve_chain)

            def norm_stats(n, chain):
                st = stats[n]
                V.tensor_tensor(diff[:], st[:, :, 1], st[:, :, 4], ALU.subtract)
                V.tensor_tensor(mean[n][:], st[:, :, 1], st[:, :, 4], ALU.add)
                chain.link(V.tensor_tensor(var[:], st[:, :, 2], st[:, :, 5], ALU.add))
                V.tensor_scalar(mean[n][:], mean[n][:], 0.5, None, ALU.mult)
                V.tensor_scalar(var[:], var[:], 1.0 / C, EPS, ALU.mult, ALU.add)
                chain.link(V.tensor_tensor(diff[:], diff[:], diff[:], ALU.mult))
                chain.link(V.scalar_tensor_tensor(out=root[:], in0=diff[:], scalar=0.25, in1=var[:],
                                                  op0=ALU.mult, op1=ALU.add))
                V.tensor_copy(var[:], root[:]).then_inc(var_ready, 1)
                dve.wait_ge(root_ready, n + 1)
                chain.link(V.reciprocal(rstd[n][:], root[:]))
                chain.link(V.tensor_tensor(diff[:], rstd[n][:], rstd[n][:], ALU.mult))
                chain.link(V.tensor_tensor(diff[:], diff[:], var[:], ALU.mult))
                chain.link(V.tensor_scalar(diff[:], diff[:], -0.5, 1.5, ALU.mult, ALU.add))
                chain.link(V.tensor_tensor(rstd[n][:], rstd[n][:], diff[:], ALU.mult))

            dve.wait_ge(c_exp_done, 1)
            chain.link(V.tensor_scalar(c_exp[:], c_exp[:], 1.0, None, ALU.add))
            chain.link(V.reciprocal(c_exp[:], c_exp[:]))
            chain.link(V.tensor_tensor(c_silu[:], c_col[:], c_exp[:], ALU.mult))
            dve.wait_ge(consts, 2)
            for b in range(B):
                last = V.tensor_scalar(c_bc[:, b, :], ones[:], c_silu[:, b:b + 1], None, ALU.mult)
            last.then_inc(c_ready, 1)
            dve.wait_ge(mod_mm, 1)
            V.tensor_copy(sa_col[:], F1[:, 0:B])
            V.tensor_scalar(ca1_col[:], F1[:, B:2 * B], 1.0, None, ALU.add)
            V.tensor_copy(bg_bc[:], F2[:, 0:E])
            for b in range(B):
                last = V.tensor_copy(mod_bc[:, b].rearrange("p k c -> p (k c)"), [S0, S1][b][:])
                last.then_inc(probs_ready, 1)
            dve.wait_ge(probs_ready, 2)
            mod = mod_bc[:]
            gates = mod_bc[:, :, 0:4:3, :]
            for b in range(B):
                gb_in = mod_bc[:, b, 0:4:3, :]
                V.tensor_scalar(gate_s[:, b], gb_in, 0.0, None, ALU.is_ge)
                last = V.tensor_scalar(gate_a[:, b], gb_in, -1.0, None, ALU.mult)
            V.tensor_scalar(mod_bc[:, :, 2, :], mod_bc[:, :, 2, :], 1.0, None, ALU.add)
            chain.link(last)
            for b in range(B):
                last = V.tensor_tensor(gate_a[:, b], gate_a[:, b], mod_bc[:, b, 0:4:3, :], ALU.max)
                V.tensor_scalar(gate_s[:, b], gate_s[:, b], 2.0, -1.0, ALU.mult, ALU.add)
            chain.link(last)
            chain.link(V.tensor_scalar(gate_a[:], gate_a[:], MOD_MIN, None, ALU.max))
            for b in range(B):
                last = V.tensor_tensor(mod_bc[:, b, 0:4:3, :], gate_a[:, b], gate_s[:, b], ALU.mult)
            chain.link(last)
            dve.wait_ge(wproj_in, 16)
            for b in range(B):
                V.tensor_tensor(wproj_b[:, b], wproj[:], mod_bc[:, b, 0], ALU.mult)
            dve.wait_ge(masks, 1)
            V.tensor_reduce(quad_head[:], block[:].rearrange("p (q a j) -> p a q j", q=QUADS, a=QUADS)[:, :, :, 0],
                            AX.X, ALU.add).then_inc(mod_ready, 1)
            V.memset(den[:, 0:1], 0.0).then_inc(y_ready, 2)
            V.memset(den[:, 1:2], 0.0).then_inc(x1_ready, 1)

            for g in range(G):
                dve.wait_ge(x_in[g], 32)
                for t in range(GT):
                    last = V.bn_stats(stats[0][:, GT * g + t, :], x_all[:, GT * g + t, :])
            chain.link(last)
            norm_stats(0, chain)
            dve.wait_ge(masks, 3)

            def front_norm(f):
                dve.wait_ge(xt_mm, f)
                for t in range(GT):
                    n = GT * f + t
                    last = V.tensor_scalar(xhat[:, t:t + 1, :], x_all[:, bass.ds(n, 1), :], mean[0][:, bass.ds(n, 1)],
                                           rstd[0][:, bass.ds(n, 1)], ALU.subtract, ALU.mult)
                last.then_inc(xhat_ready, 1)

            def front_elu(f, par):
                dve.wait_ge(eq_ready, f + 1)
                V.scalar_tensor_tensor(out=q_t[par][:], in0=F1[:], scalar=0.0, in1=exp_q[:], op0=ALU.max,
                                       op1=ALU.add).then_inc(q_ready, 1)
                dve.wait_ge(ek_ready, f + 1)
                V.scalar_tensor_tensor(out=k_t[par][:], in0=F2[:], scalar=0.0, in1=exp_k[:], op0=ALU.max,
                                       op1=ALU.add).then_inc(k_ready, 1)

            def front_z(f, par, chain, first=False):
                dve.wait_ge(k_ready, f + 1)
                for b in range(B):
                    cols = slice(2 * P * b, 2 * P * b + 2 * P)
                    start = 0.0 if first else z_t[1 - par][:, 2 * P * b + 2 * P - 1:2 * P * b + 2 * P]
                    last = V.tensor_tensor_scan(z_t[par][:, cols], ones[:, 0:1].broadcast_to([P, 2 * P]),
                                                k_t[par][:, cols], start, ALU.mult, ALU.add)
                chain.link(last)
                V.tensor_tensor(qz[:], z_t[par][:], q_t[par][:], ALU.mult).then_inc(qz_ready, 1)

            def front_rden(f, par, chain):
                dve.wait_ge(den_mm, f + 1)
                chain.link(V.tensor_scalar(den[:], F2[:], DEN_EPS, None, ALU.add))
                V.reciprocal(rden[par][:], den[:]).then_inc(rden_ready, 1)

            def core_probs(g, s, b):
                dve.wait_ge(y_mm, 1 + 4 * g + 2 * s)
                for q in range(QUADS):
                    dve.wait_ge(score_mm, 16 * g + 8 * s + 4 * b + q + 1)
                    V.tensor_tensor(probs[:, b, q, :], score_bank[q % 2][:, 0:QUADS * L],
                                    causal[:].rearrange("p a t -> p (a t)"), ALU.mult).then_inc(probs_ready, 1)

            def core_state(g, u):
                dve.wait_ge(kv_mm, 4 * g + u + 1)
                V.tensor_tensor(state[:, u % 2], ST[:, 0:2 * P].rearrange("p (b c) -> p b c", b=B),
                                block[:].unsqueeze(1).broadcast_to([P, B, P]), ALU.mult).then_inc(state_ready, 1)

            def core_y(g, par, u):
                s, half = u // 2, u % 2
                dve.wait_ge(y_mm, 4 * g + u + 2)
                r = rden[par][:].rearrange("p (b s h t) -> p b s h t", b=B, s=2, h=2)[:, :, s, half, :]
                V.tensor_tensor(y_n[:, s, :, L * half:L * half + L],
                                y_bank[half][:, 0:2 * L].rearrange("p (b t) -> p b t", b=B), r,
                                ALU.mult).then_inc(y_ready, 1)

            def core_x1(g, chain):
                dve.wait_ge(proj_mm, g + 1)
                rows = x_all[:, bass.ds(GT * g, GT), :]
                x1 = V.tensor_tensor(rows, rows, F0[:].rearrange("p (t c) -> p t c", t=GT), ALU.add)
                x1.then_inc(x1_ready, 1)
                dve.wait_ge(x1_ready, g + 2)
                for t in range(GT):
                    n = GT * g + t
                    V.bn_stats(stats[1][:, bass.ds(n, 1), :].rearrange("p o k -> p (o k)"), x_all[:, bass.ds(n, 1), :])

            def step(g, par, chain, front=True, more=True):
                f, fpar = g + 1, 1 - par
                if front:
                    front_norm(f)
                core_probs(g, 0, 0)
                core_state(g, 1)
                core_probs(g, 0, 1)
                if front:
                    front_elu(f, fpar)
                core_y(g, par, 0)
                core_state(g, 2)
                core_y(g, par, 1)
                core_probs(g, 1, 0)
                if front:
                    front_z(f, fpar, chain)
                core_state(g, 3)
                core_probs(g, 1, 1)
                if front:
                    front_rden(f, fpar, chain)
                core_y(g, par, 2)
                if more:
                    core_state(g, 4)
                core_y(g, par, 3)
                core_x1(g, chain)

            front_norm(0)
            front_elu(0, 0)
            front_z(0, 0, chain, True)
            front_rden(0, 0, chain)
            core_state(0, 0)
            before = chain.n
            with dve.Fori(0, G // 2 - 1) as k:
                step(2 * k, 0, Count(dve, dve_chain, before + 4 * k))
                step(2 * k + 1, 1, Count(dve, dve_chain, before + 4 * k + 2))
            chain.n = before + 4 * (G // 2 - 1)
            step(G - 2, 0, chain)
            step(G - 1, 1, chain, front=False, more=False)

            chain.link(V.memset(den[:, 0:1], 0.0))
            norm_stats(1, chain)
            before = chain.n

            def second_norm(g, par, chain):
                if not isinstance(g, int):
                    dve.wait_ge(h2t_mm, g - 1)
                    dve.wait_ge(h2_kept, g - 1)
                for t in range(GT):
                    n = GT * g + t
                    last = V.tensor_scalar(h2_s[par][:, t:t + 1, :], x_all[:, bass.ds(n, 1), :],
                                           mean[1][:, bass.ds(n, 1)], rstd[1][:, bass.ds(n, 1)],
                                           ALU.subtract, ALU.mult)
                chain.link(last)
                for b in range(B):
                    rows = h2_s[par][:, 2 * b:2 * b + 2, :]
                    last = V.tensor_tensor(rows, rows, mod_bc[:, b, 2:3, :].broadcast_to([P, 2, C]), ALU.mult)
                chain.link(last)
                for b in range(B):
                    rows = h2_s[par][:, 2 * b:2 * b + 2, :]
                    last = V.tensor_tensor(rows, rows, mod_bc[:, b, 1:2, :].broadcast_to([P, 2, C]), ALU.add)
                last.then_inc(h2_ready, 1)

            second_norm(0, 0, chain)
            second_norm(1, 1, chain)
            with dve.Fori(1, G // 2) as k:
                second_norm(2 * k, 0, Count(dve, dve_chain, before + 4 * k))
                second_norm(2 * k + 1, 1, Count(dve, dve_chain, before + 4 * k + 2))
            chain.n = before + 2 * G

            dve.wait_ge(logit_mm, G)
            dve.wait_ge(masks, 8)
            chain.link(V.tensor_tensor(logit[:], S0[:, 0:NT * E].rearrange("p (n e) -> p n e", e=E),
                                       bg_bc[:].unsqueeze(1).broadcast_to([P, NT, E]), ALU.add))
            chain.link(V.tensor_reduce(best[:], logit[:], AX.X, ALU.max))
            chain.link(V.tensor_tensor(logit[:], logit[:], best[:].unsqueeze(2).broadcast_to([P, NT, E]), ALU.is_ge))
            chain.link(V.tensor_tensor(logit[:], logit[:], prefer[:], ALU.mult))
            chain.link(V.tensor_reduce(best[:], logit[:], AX.X, ALU.max))
            V.tensor_tensor(onehot[:], logit[:], best[:].unsqueeze(2).broadcast_to([P, NT, E]),
                            ALU.is_equal).then_inc(onehot_ready, 1)
            dve.wait_ge(rank_mm, 1)
            chain.link(V.tensor_copy(tot[:], F1[:, 0:NT * E].rearrange("p (n e) -> p e n", e=E)))
            V.tensor_reduce(cnt[:], tot[:], AX.X, ALU.add)
            chain.link(V.tensor_tensor_scan(cum[:].rearrange("p e n -> p (e n)"),
                                            ones[:, 0:1].broadcast_to([P, E * NT]),
                                            tot[:].rearrange("p e n -> p (e n)"), 0.0, ALU.mult, ALU.add))
            chain.link(V.tensor_tensor(r_cmp[:], cnt[:].unsqueeze(2).broadcast_to([P, E, NT]), iota_tok[:], ALU.is_gt))
            chain.link(V.tensor_reduce(tiles_e[:], r_cmp[:], AX.X, ALU.add))
            chain.link(V.tensor_tensor_scan(tiles_cum[:], ones[:, 0:1].broadcast_to([P, E]), tiles_e[:], 0.0,
                                            ALU.mult, ALU.add))
            V.tensor_tensor(t_cmp[:], tiles_cum[0:1, :].unsqueeze(1).broadcast_to([1, SLOT_TILES, E]), iota_tile[:],
                            ALU.is_le)
            chain.link(V.tensor_tensor(base_e[:], tiles_cum[:], tiles_e[:], ALU.subtract))
            chain.link(V.scalar_tensor_tensor(out=base_e[:], in0=base_e[:], scalar=float(P), in1=cum[:, :, NT - 1],
                                              op0=ALU.mult, op1=ALU.subtract))
            chain.link(V.tensor_tensor(base_e[:], base_e[:], cnt[:], ALU.add))
            chain.link(V.tensor_tensor(cum[:], cum[:], tot[:], ALU.subtract))
            chain.link(V.tensor_tensor(cum[:], cum[:], base_e[:].unsqueeze(2).broadcast_to([P, E, NT]), ALU.add))
            chain.link(V.tensor_tensor(logit[:], F0[:, 0:NT * E].rearrange("p (n e) -> p n e", e=E),
                                       cum[:].rearrange("p e n -> p n e"), ALU.add))
            chain.link(V.tensor_tensor(logit[:], logit[:], onehot[:], ALU.mult))
            chain.link(V.tensor_reduce(slot_f[:], logit[:], AX.X, ALU.add))
            V.tensor_copy(slot_i[:], slot_f[:])
            chain.link(V.tensor_reduce(t_exp[:], t_cmp[:], AX.X, ALU.add))
            chain.link(V.tensor_scalar(t_exp[:], t_exp[:], float(E - 1), None, ALU.min))
            V.tensor_copy(t_expert[:], t_exp[:]).then_inc(slots_ready, 1)
            dve.wait_ge(slots_ready, 1)

            dve.wait_ge(w1_in, 16)

            def pick_w1(n, par, first=False):
                e = dve.value_load(t_expert[0:1, bass.ds(n, 1)], min_val=0, max_val=E - 1)
                if not first:
                    dve.wait_ge(up_mm, n - 1)
                V.tensor_copy(w1_cur[par][:], w1_all[:, bass.ds(e, 1)].rearrange("p o h -> p (o h)")
                              ).then_inc(w1c_ready, 1)

            def columns(n, par):
                dve.wait_ge(row_mm, n + 1)
                V.tensor_copy(h_col[par][:], [F0, F1][par][:, 0:P]).then_inc(col_ready, 1)

            def rows_out(n, par, k, first=False):
                dve.wait_ge(down_mm, n + 1)
                if not first:
                    dve.wait_ge(row_out[par], 16 * k)
                V.tensor_copy(y_row[par][:], [Y0, Y1][par][:, 0:C]).then_inc(yrow_ready, 1)

            pick_w1(0, 0, True)
            columns(0, 0)
            pick_w1(1, 1, True)
            columns(1, 1)
            rows_out(0, 0, 0, True)
            pick_w1(2, 0)
            columns(2, 0)
            rows_out(1, 1, 0, True)
            with dve.Fori(1, SLOT_TILES // 2 - 1) as k:
                pick_w1(2 * k + 1, 1)
                columns(2 * k + 1, 1)
                rows_out(2 * k, 0, k)
                pick_w1(2 * k + 2, 0)
                columns(2 * k + 2, 0)
                rows_out(2 * k + 1, 1, k)
            last_k = SLOT_TILES // 2 - 1
            pick_w1(2 * last_k + 1, 1)
            columns(2 * last_k + 1, 1)
            rows_out(2 * last_k, 0, last_k)
            rows_out(2 * last_k + 1, 1, last_k)

            for g in range(G):
                dve.wait_ge(gathered[g], 16 * GT)
                for b in range(B):
                    rows = slice(GT * g + 2 * b, GT * g + 2 * b + 2)
                    last = V.tensor_tensor(h2_all[:, rows], h2_all[:, rows],
                                           mod_bc[:, b, 3:4, :].broadcast_to([P, 2, C]), ALU.mult)
                chain.link(last)
                V.tensor_tensor(x_all[:, GT * g:GT * g + GT], x_all[:, GT * g:GT * g + GT],
                                h2_all[:, GT * g:GT * g + GT], ALU.add).then_inc(out_ready, 1)

        @blk.tensor
        def _(pe):
            mm = nc.tensor.matmul
            pe.wait_ge(c_ready, 1)
            pe.wait_ge(wmod_in, 16)
            pe.wait_ge(wgate_in, 32)
            pe.wait_ge(consts, 2)
            for k in range(2):
                mm(F1[:, B * k:B * k + B], wmod_sb[:, k * C:(k + 1) * C], c_silu[:], start=True, stop=True)
            mm(F2[:, 0:E], ones[0:1, :], bg_row[:], start=True, stop=True)
            for b in range(B):
                mm([S0, S1][b][:], c_bc[:, b, :], wmod_sb[:, 2 * C:6 * C], start=True, stop=True)
            pe.wait_ge(pool_chain, 1)
            mm(ST[:, 0:2 * P], zeros[:, 0:P], zeros[:], start=True, stop=True).then_inc(kv_mm, 1)
            mm(ST[:, 0:P], zeros[:, 0:P], zeros[:, 0:P], start=False, stop=True,
               skip_group_check=True).then_inc(y_mm, 1)
            mm(ST[:, 0:2 * P], zeros[:, 0:P], zeros[:], start=False, stop=True,
               skip_group_check=True).then_inc(mod_mm, 1)
            pe.wait_ge(wqkv_in, 16)

            def front_x(f):
                pe.wait_ge(xhat_ready, f + 1)
                pe.wait_ge(v_ready, f)
                if not isinstance(f, int) or f >= 1:
                    pe.wait_ge(x1_ready, f)
                for t in range(GT):
                    last = nc.tensor.transpose(F0[:, t * P:(t + 1) * P], xhat[:, t, :], ident[:])
                last.then_inc(xt_mm, 1)

            def front_qkv(f):
                pe.wait_ge(ht_ready, f + 1)
                pe.wait_ge(kn_ready, f)
                mm(F1[:], wqkv[:, 0:C], h_t[:], start=True, stop=True).then_inc(q_mm, 1)
                pe.wait_ge(rden_ready, f)
                mm(F2[:], wqkv[:, C:2 * C], h_t[:], start=True, stop=True).then_inc(k_mm, 1)
                for t in range(GT):
                    last = mm(F0[:, t * P:(t + 1) * P], h_t[:, t * P:(t + 1) * P], wqkv[:, 2 * C:3 * C],
                              start=True, stop=True)
                last.then_inc(v_mm, 1)

            def front_kt(f, par):
                pe.wait_ge(k_ready, f + 1)
                for t in range(GT):
                    last = nc.tensor.transpose(F1[:, t * P:(t + 1) * P], k_t[par][:, t * P:(t + 1) * P], ident[:])
                last.then_inc(kt_mm, 1)

            def front_den(f):
                pe.wait_ge(qz_ready, f + 1)
                mm(F2[:], block[:], qz[:], start=True, stop=True).then_inc(den_mm, 1)

            def core_scores(g, par, s, b):
                t = 2 * b + s
                if s == 0 and b == 0:
                    pe.wait_ge(qm_ready, g + 1)
                for q in range(QUADS):
                    pe.wait_ge(probs_ready, 16 * g + 8 * s + 4 * b + q + 1)
                    rows = slice(32 * q, 32 * q + 32)
                    for half in range(2):
                        tok = t * P + half * L
                        last = mm(score_bank[q % 2][L * half:L * half + L, 0:QUADS * L], k_t[par][rows, tok:tok + L],
                                  q_m[par][rows, 2 * t + half].rearrange("p a t -> p (a t)"), start=True, stop=True)
                    last.then_inc(score_mm, 1)

            def core_across(g, par, u):
                s, half = u // 2, u % 2
                pe.wait_ge(state_ready, 4 * g + u + 1)
                pe.wait_ge(y_ready, 4 * g + u + 1)
                for b in range(B):
                    tok = (2 * b + s) * P + half * L
                    mm(y_bank[half][:, b * L:b * L + L], state[:, half, b, :], q_t[par][:, tok:tok + L],
                       start=(b == 0), stop=False, skip_group_check=True)
                if u == 0:
                    pe.wait_ge(kn_ready, g + 1)
                    pe.wait_ge(v_ready, g + 1)
                rows = slice(L * half, L * half + L)
                for b in range(B):
                    last = mm(ST[:, b * P:(b + 1) * P], k_n[par][rows, 2 * b + s, :], v_n[par][rows, 2 * b + s, :],
                              start=False, stop=True, skip_group_check=True)
                last.then_inc(kv_mm, 1)

            def core_within(g, par, u):
                s, half = u // 2, u % 2
                masked = 2 + 16 * g + 8 * s + 8
                masked = masked if isinstance(masked, int) else pe.to_reg(masked)
                pe.wait_ge(masks, 5)
                pe.wait_ge(probs_ready, masked)
                rows = slice(L * half, L * half + L)
                for b in range(B):
                    for a in range(QUADS):
                        for q in range(QUADS):
                            last = mm(y_bank[half][32 * q:32 * q + 32, b * L:b * L + L],
                                      v_m[par][rows, 2 * b + s, C * a + 32 * q:C * a + 32 * q + 32],
                                      probs[rows, b, q, a * L:a * L + L], start=False, stop=(a == QUADS - 1),
                                      skip_group_check=True)
                last.then_inc(y_mm, 1)

            def core_proj(g, front):
                pe.wait_ge(v_ready, g + 2 if front else g + 1)
                pe.wait_ge(y_ready, 2 + 4 * g + 4)
                for t in range(GT):
                    last = mm(F0[:, t * P:(t + 1) * P], y_n[:, t % 2, t // 2, :], wproj_b[:, t // 2, :],
                              start=True, stop=True)
                last.then_inc(proj_mm, 1)

            def step(g, par, front=True):
                f, fpar = g + 1, 1 - par
                core_scores(g, par, 0, 0)
                if front:
                    front_x(f)
                core_across(g, par, 0)
                core_scores(g, par, 0, 1)
                if front:
                    front_qkv(f)
                core_within(g, par, 0)
                core_across(g, par, 1)
                core_within(g, par, 1)
                core_scores(g, par, 1, 0)
                if front:
                    front_kt(f, fpar)
                core_across(g, par, 2)
                core_scores(g, par, 1, 1)
                if front:
                    front_den(f)
                core_within(g, par, 2)
                core_across(g, par, 3)
                core_within(g, par, 3)
                core_proj(g, front)

            front_x(0)
            front_qkv(0)
            front_kt(0, 0)
            front_den(0)
            with pe.Fori(0, G // 2 - 1) as k:
                step(2 * k, 0)
                step(2 * k + 1, 1)
            step(G - 2, 0)
            step(G - 1, 1, front=False)

            def gate_turn(g, par):
                pe.wait_ge(h2_ready, g + 1)
                for t in range(GT):
                    last = nc.tensor.transpose([F0, F1][par][:, t * P:(t + 1) * P], h2_s[par][:, t, :], ident[:])
                last.then_inc(h2t_mm, 1)

            def gate_logits(g, par):
                pe.wait_ge(h2t_ready, g + 1)
                for t in range(GT):
                    last = mm(S0[:, bass.ds((GT * g + t) * E, E)], h2_t[par][:, t * P:(t + 1) * P], wg_sb[:],
                              start=True, stop=True)
                last.then_inc(logit_mm, 1)

            pe.wait_ge(x1_ready, G + 1)
            with pe.Fori(0, G // 2) as k:
                for par in range(2):
                    gate_turn(2 * k + par, par)
                    gate_logits(2 * k + par, par)

            pe.wait_ge(onehot_ready, 1)
            hot = onehot[:].rearrange("p n e -> p (n e)")
            mm(F0[:, 0:NT * E], upper[:], hot, start=True, stop=True)
            mm(F1[:, 0:NT * E], ones[:], hot, start=True, stop=True).then_inc(rank_mm, 1)
            pe.wait_ge(slots_ready, 1)

            def expert_up(n, par, k):
                pe.wait_ge(row_in[par], 16 * (k + 1))
                nc.tensor.transpose([F0, F1][par][:, 0:P], h_row[par][:], ident[:]).then_inc(row_mm, 1)
                pe.wait_ge(w1c_ready, n + 1)
                pe.wait_ge(col_ready, n + 1)
                for j in range(HC):
                    last = mm([S0, S1][par][:, j * P:(j + 1) * P], w1_cur[par][:, j * P:(j + 1) * P], h_col[par][:],
                              start=True, stop=True)
                last.then_inc(up_mm, 1)

            def expert_down(n, par):
                pe.wait_ge(gelu_ready, n + 1)
                pe.wait_ge(w2c_ready, n + 1)
                for j in range(HC):
                    last = mm([Y0, Y1][par][:, 0:C], gelu[par][:, j, :], w2_cur[par][:, j, :], start=(j == 0),
                              stop=(j == HC - 1))
                last.then_inc(down_mm, 1)

            expert_up(0, 0, 0)
            expert_up(1, 1, 0)
            expert_down(0, 0)
            with pe.Fori(1, SLOT_TILES // 2) as k:
                expert_up(2 * k, 0, k)
                expert_down(2 * k - 1, 1)
                expert_up(2 * k + 1, 1, k)
                expert_down(2 * k, 0)
            expert_down(SLOT_TILES - 1, 1)


_INS = ['L0_attn_x', 'L0_attn_w_attn', 'L0_attn_w_proj', 'L0_ffn_W1', 'L0_ffn_W2', 'L0_ffn_Wg', 'L0_ffn_bg', 'L0_c',
        'L0_wmod']
_OUTS = [((2, 2048, 128), 'float32')]


def kernel(**inputs):
    import numpy as _np
    import concourse.bacc as _bacc
    from concourse import mybir as _mybir
    from concourse.bass_utils import run_bass_kernel_spmd as _run

    nc = _bacc.Bacc("TRN2", target_bir_lowering=False, num_devices=1)
    arrays, args = {}, []
    for name in _INS:
        a = _np.ascontiguousarray(inputs[name])
        arrays[f"in_{name}_dram"] = a
        args.append(nc.dram_tensor(f"in_{name}_dram", a.shape, _mybir.dt.from_np(a.dtype), kind="ExternalInput").ap())
    for i, (shape, dtype) in enumerate(_OUTS):
        dt = _mybir.dt.from_np(_np.dtype(dtype))
        args.append(nc.dram_tensor(f"out_{i}_dram", shape, dt, kind="ExternalOutput").ap())
    build(nc, *args)
    r = _run(nc, [arrays], core_ids=[0])
    got = tuple(r.results[0][f"out_{i}_dram"] for i in range(len(_OUTS)))
    return got[0]
```

```python
from contextlib import ExitStack

import concourse.bass as bass
from concourse import mybir

F32 = mybir.dt.float32
I32 = mybir.dt.int32
ALU = mybir.AluOpType
ACT = mybir.ActivationFunctionType
AX = mybir.AxisListType

B, T, C = 2, 2048, 128
HEADS, HD = 16, 8
E, HID = 8, 512
P = 128
NT = B * T // P
GT = 4
G = NT // GT
L = 64
HC = HID // P
SLOT_TILES = NT + E - 1
EXPERT_TILES = NT + 1
REGION = EXPERT_TILES * P
QUADS = 4
ROW = 2 * C + 8
NO_TOKEN = 8192
RING = 6
WBUFS = 3
ROUNDS = -(-SLOT_TILES // RING)
EPS = 1e-5
DEN_EPS = 1e-6
MOD_MIN = 0.25


def wait_ge(eng, sem, value):
    if not isinstance(value, int) or value > 0:
        eng.wait_ge(sem, value)


class Count:

    def __init__(self, eng, sem, before=0):
        self.eng, self.sem, self.before, self.n = eng, sem, before, 0

    def link(self, ins):
        self.n += 1
        ins.then_inc(self.sem, 1)
        self.eng.wait_ge(self.sem, self.before + self.n)


def build(nc, x, w_attn, w_proj, w1, w2, wg, bg, c, wmod, out):
    sorted_rows = nc.dram_tensor("sorted_rows", ((E * EXPERT_TILES + 1) * P, ROW), F32, kind="Internal").ap()

    with ExitStack() as ctx:
        def sb(name, shape, dt=F32):
            return ctx.enter_context(nc.sbuf_tensor(name, shape, dt))

        def sem(name):
            return ctx.enter_context(nc.semaphore(name))

        x_all = sb("x_all", [P, NT, C])
        row_buf = [sb(f"row_buf{n}", [P, GT, ROW]) for n in range(2)]
        w1_all = sb("w1_all", [P, E, HID])
        w2_all = sb("w2_all", [P, E, HC, C])
        wqkv = sb("wqkv", [P, 3 * C])
        wproj = sb("wproj", [P, C])
        wproj_b = sb("wproj_b", [P, B, C])
        wg_sb = sb("wg_sb", [P, E])
        bg_row = sb("bg_row", [1, E])
        bg_bc = sb("bg_bc", [P, E])
        wmod_sb = sb("wmod_sb", [P, 6 * C])
        c_col = sb("c_col", [P, B])
        c_exp = sb("c_exp", [P, B])
        c_silu = sb("c_silu", [P, B])
        c_bc = sb("c_bc", [P, B, P])
        sa_col = sb("sa_col", [P, B])
        ca1_col = sb("ca1_col", [P, B])
        mod_bc = sb("mod_bc", [P, B, 4, C])
        gate_a = sb("gate_a", [P, B, 2, C])
        gate_s = sb("gate_s", [P, B, 2, C])
        ident = sb("ident", [P, P])
        ones = sb("ones", [P, P])
        zeros = sb("zeros", [P, ROW])
        upper = sb("upper", [P, P])
        block = sb("block", [P, P])
        quad_head = sb("quad_head", [P, QUADS])
        causal = sb("causal", [P, QUADS, L])
        iota_tok = sb("iota_tok", [1, E, NT])
        iota_tile = sb("iota_tile", [1, ROUNDS * RING, E])
        prefer = sb("prefer", [P, GT, E])
        stats = sb("stats", [P, NT, 6])
        mean = sb("mean", [P, NT])
        var = sb("var", [P, NT])
        diff = sb("diff", [P, NT])
        root = sb("root", [P, NT])
        rstd, shift = sb("rstd", [P, NT]), sb("shift", [P, NT])
        minus_half = sb("minus_half", [P, GT])
        stats2 = sb("stats2", [P, GT, 6])
        mean2, diff2, var2, guess2, newton2, rstd2 = (
            sb(n, [P, GT]) for n in ("mean2", "diff2", "var2", "guess2", "newton2", "rstd2"))
        xhat = sb("xhat", [P, GT, C])
        h_t = sb("h_t", [P, GT * P])
        relu_q = sb("relu_q", [P, GT * P])
        relu_k = sb("relu_k", [P, GT * P])
        exp_q = sb("exp_q", [P, GT * P])
        exp_k = sb("exp_k", [P, GT * P])
        q_t = [sb(f"q_t{n}", [P, GT * P]) for n in range(2)]
        k_t = [sb(f"k_t{n}", [P, GT * P]) for n in range(2)]
        k_q = [sb(f"k_q{n}", [P, QUADS, GT * P]) for n in range(2)]
        q_m = [sb(f"q_m{n}", [P, QUADS, GT * P]) for n in range(2)]
        k_n = [sb(f"k_n{n}", [P, GT, C]) for n in range(2)]
        v_n = [sb(f"v_n{n}", [P, GT, C]) for n in range(2)]
        v_m = [sb(f"v_m{n}", [P, GT, QUADS * (P + HD)]) for n in range(2)]
        z_t = [sb(f"z_t{n}", [P, GT * P]) for n in range(2)]
        qz = sb("qz", [P, GT * P])
        den = sb("den", [P, GT * HEADS])
        den_inv = sb("den_inv", [P, GT * HEADS])
        rden = [sb(f"rden{n}", [P, GT * P]) for n in range(2)]
        probs = sb("probs", [P, 2, B, QUADS, QUADS * L])
        state = sb("state", [P, 2, B, C])
        y_n = sb("y_n", [P, 2, B, P])
        h2_t = sb("h2_t", [P, GT * P])
        logit = sb("logit", [P, GT, E])
        best = sb("best", [P, GT])
        onehot = sb("onehot", [P, GT, E])
        counts = sb("counts", [P, E, GT + 1])
        carry = sb("carry", [P, E, GT + 1])
        place = sb("place", [P, E, GT + 1])
        pick_row = sb("pick_row", [P, GT, E])
        slot_f = sb("slot_f", [P, GT])
        slot_i = [sb(f"slot_i{n}", [P, GT], I32) for n in range(2)]
        region = sb("region", [1, E])
        tail_i = sb("tail_i", [1, E], I32)
        cnt = sb("cnt", [1, E])
        r_cmp = sb("r_cmp", [1, E, NT])
        tiles_e = sb("tiles_e", [1, E])
        tiles_cum = sb("tiles_cum", [1, E])
        t_cmp = sb("t_cmp", [1, ROUNDS * RING, E])
        t_skip = sb("t_skip", [1, ROUNDS * RING, E])
        t_exp = sb("t_exp", [1, ROUNDS * RING])
        t_row = sb("t_row", [1, ROUNDS * RING])
        code = sb("code", [1, ROUNDS])
        t_row_i = sb("t_row_i", [1, ROUNDS * RING], I32)
        t_code = sb("t_code", [1, ROUNDS], I32)
        slot_row = [v_m[0][:, n // 2, n % 2 * ROW:(n % 2 + 1) * ROW] for n in range(RING)]
        gelu = [v_m[1][:, n, 0:HID].rearrange("p (k c) -> p k c", k=HC) for n in range(2)]
        flat_q = [q_m[n][:].rearrange("p a t -> p (a t)") for n in range(2)]
        y_row = [flat_q[0][:, n * C:(n + 1) * C] for n in range(RING)]
        gb_sel, y_gated, h_col = ([flat_q[1][:, (2 * i + n) * P:(2 * i + n + 1) * P] for n in range(2)]
                                  for i in range(3))
        w1_cur = [k_q[0][:, n, :] for n in range(WBUFS)]
        w2_cur = [k_q[1][:, n, :].rearrange("p (k c) -> p k c", k=HC) for n in range(WBUFS)]
        slot_token = [sb(f"slot_token{n}", [P, 1], I32) for n in range(RING)]
        gb_diff = sb("gb_diff", [P, C])

        bank = [ctx.enter_context(nc.psum_tensor(f"bank{n}", [P, 512], F32)) for n in range(8)]
        F0, F1, F2, S0, S1, ST, Y0, Y1 = bank
        score_bank, y_bank = [S0, S1], [Y0, Y1]
        LOGIT, RANK, TOTAL = (F0[:, i * GT * E:(i + 1) * GT * E] for i in range(3))

        x_in = [sem(f"x_in{g}") for g in range(G)]
        c_in, wmod_in, wqkv_in, wproj_in, wgate_in, w1_in, w2_in = (
            sem(n) for n in ("c_in", "wmod_in", "wqkv_in", "wproj_in", "wgate_in", "w1_in", "w2_in"))
        consts, masks = sem("consts"), sem("masks")
        c_exp_done, c_ready, mod_mm, mod_ready = (sem(n) for n in ("c_exp_done", "c_ready", "mod_mm", "mod_ready"))
        var_ready, root_ready, norm_ready = sem("var_ready"), sem("root_ready"), sem("norm_ready")
        dve_chain, act_chain, pool_chain = sem("dve_chain"), sem("act_chain"), sem("pool_chain")
        xhat_ready, xt_mm, ht_ready = sem("xhat_ready"), sem("xt_mm"), sem("ht_ready")
        q_mm, k_mm, v_mm, kt_mm, den_mm = (sem(n) for n in ("q_mm", "k_mm", "v_mm", "kt_mm", "den_mm"))
        eq_ready, ek_ready, q_ready, k_ready, qm_ready = (
            sem(n) for n in ("eq_ready", "ek_ready", "q_ready", "k_ready", "qm_ready"))
        v_ready, kn_ready, kq_ready, qz_ready, inv_ready, inv_mm, rden_ready = (
            sem(n) for n in ("v_ready", "kn_ready", "kq_ready", "qz_ready", "inv_ready", "inv_mm", "rden_ready"))
        score_mm, probs_ready = sem("score_mm"), sem("probs_ready")
        kv_mm, state_ready, y_mm, y_ready = (sem(n) for n in ("kv_mm", "state_ready", "y_mm", "y_ready"))
        proj_mm, x1_ready = sem("proj_mm"), sem("x1_ready")
        var2_ready, guess2_ready, norm2_ready, centred, plain_ready = (
            sem(n) for n in ("var2_ready", "guess2_ready", "norm2_ready", "centred", "plain_ready"))
        h2_ready, h2t_mm, h2t_ready, logit_mm, onehot_ready, rank_mm, slots_ready = (
            sem(n) for n in ("h2_ready", "h2t_mm", "h2t_ready", "logit_mm", "onehot_ready", "rank_mm",
                             "slots_ready"))
        scattered = [sem(f"scattered{n}") for n in range(2)]
        tails_ready, table_ready, closed = sem("tails_ready"), sem("table_ready"), sem("closed")
        row_in = [sem(f"row_in{n}") for n in range(RING)]
        row_mm, col_ready, w1c_ready, w2c_ready, up_mm, gelu_ready, down_mm, gated_ready, yrow_ready = (
            sem(n) for n in ("row_mm", "col_ready", "w1c_ready", "w2c_ready", "up_mm", "gelu_ready", "down_mm",
                             "gated_ready", "yrow_ready"))
        row_out = [sem(f"row_out{n}") for n in range(RING)]

        def close_runs(eng, queue_experts):
            eng.wait_ge(tails_ready, 1)
            for e in queue_experts:
                row = eng.value_load(tail_i[0:1, e:e + 1], min_val=e * REGION, max_val=e * REGION + NT * P)
                eng.dma_start(sorted_rows[bass.ds(row, P)], zeros[:]).then_inc(closed, 16)

        x_v = x.rearrange("b (g s p) c -> b g p s c", s=2, p=P)
        out_rows = out.rearrange("b t c -> (b t) c")
        sorted_v = sorted_rows.rearrange("(n p) c -> n p c", p=P)

        blk = ctx.enter_context(nc.Block())

        @blk.sync
        def _(sp):
            with nc.allow_non_contiguous_dma(reason="256 values of c, by column"):
                sp.dma_start(c_col[:], c.rearrange("b c -> c b")).then_inc(c_in, 16)
            sp.dma_start(wmod_sb[:], wmod).then_inc(wmod_in, 16)
            for g in range(G):
                for b in range(B):
                    sp.dma_start(x_all[:, GT * g + 2 * b:GT * g + 2 * b + 2, :], x_v[b, g]).then_inc(x_in[g], 16)
            sp.dma_start(w1_all[:], w1.rearrange("e d h -> d e h")).then_inc(w1_in, 16)
            sp.dma_start(w2_all[:], w2.rearrange("e (k p) d -> p e k d", p=P)).then_inc(w2_in, 16)

            close_runs(sp, range(0, E, 2))

            sp.wait_ge(table_ready, 1)
            sp.wait_ge(closed, 16 * E)
            for n in range(2):
                sp.wait_ge(scattered[n], 16 * (NT // 2 + n))

            def load(n, ring):
                tile = sp.value_load(t_row_i[0:1, n:n + 1] if isinstance(n, int) else t_row_i[0:1, bass.ds(n, 1)],
                                     min_val=0, max_val=E * EXPERT_TILES)
                wait_ge(sp, yrow_ready, n - RING + 1)
                sp.dma_start(slot_row[ring], sorted_v[bass.ds(tile, 1)].rearrange("o p c -> p (o c)")
                             ).then_inc(row_in[ring], 16)

            for ring in range(RING):
                load(ring, ring)
            with sp.Fori(1, ROUNDS - 1) as k:
                for ring in range(RING):
                    load(RING * k + ring, ring)
            for n in range(RING * (ROUNDS - 1), SLOT_TILES):
                load(n, n % RING)
            for ring in range(RING):
                sp.wait_ge(row_out[ring], 16 * len(range(ring, SLOT_TILES, RING)))

        @blk.gpsimd
        def _(pool):
            chain = Count(pool, pool_chain)
            chain.link(nc.gpsimd.memset(zeros[:], 0.0))
            pool.dma_start(sorted_v[E * EXPERT_TILES], zeros[:]).then_inc(scattered[1], 16)
            chain.link(nc.gpsimd.memset(ident[:], 0.0))
            nc.gpsimd.affine_select(out=ident[:], in_=ident[:], compare_op=ALU.not_equal, fill=1.0, base=0,
                                    pattern=[[-1, P]], channel_multiplier=1).then_inc(consts, 1)
            chain.link(nc.gpsimd.memset(ones[:], 1.0))
            nc.gpsimd.affine_select(out=upper[:], in_=ones[:], compare_op=ALU.is_gt, fill=0.0, base=0,
                                    pattern=[[1, P]], channel_multiplier=-1).then_inc(consts, 1)
            bl = block[:].rearrange("p (h j) -> p h j", j=HD)
            chain.link(nc.gpsimd.affine_select(out=bl, in_=ones[:].rearrange("p (h j) -> p h j", j=HD),
                                               compare_op=ALU.is_ge, fill=0.0, base=0,
                                               pattern=[[-HD, HEADS], [0, HD]], channel_multiplier=1))
            nc.gpsimd.affine_select(out=bl, in_=bl, compare_op=ALU.is_ge, fill=0.0, base=HD - 1,
                                    pattern=[[HD, HEADS], [0, HD]], channel_multiplier=-1).then_inc(masks, 1)
            chain.link(nc.gpsimd.memset(causal[:], 1.0))
            for half in range(2):
                rows = slice(L * half, L * half + L)
                nc.gpsimd.affine_select(out=causal[rows], in_=causal[rows], compare_op=ALU.is_ge, fill=0.0, base=0,
                                        pattern=[[0, QUADS], [1, L]], channel_multiplier=-1).then_inc(masks, 1)
                pool.wait_ge(masks, 2 + half)
            for n in range(2):
                nc.gpsimd.memset(v_m[n][:], 0.0).then_inc(masks, 1)
            for n in range(2):
                nc.gpsimd.memset(k_q[n][:], 0.0).then_inc(masks, 1)
            for n in range(2):
                chain.link(nc.gpsimd.memset(row_buf[n][:, :, 2 * C:ROW], 0.0))
                meta = row_buf[n][:].rearrange("p (b s) r -> p b s r", b=B)
                chain.link(nc.gpsimd.iota(meta[:, :, :, 2 * C], pattern=[[T, B], [P, 2]],
                                          base=-NO_TOKEN - n * 2 * P, channel_multiplier=1,
                                          allow_small_or_imprecise_dtypes=True))
                chain.link(nc.gpsimd.iota(meta[:, :, :, 2 * C + 1], pattern=[[1, B], [0, 2]], base=0,
                                          channel_multiplier=0, allow_small_or_imprecise_dtypes=True))
            nc.gpsimd.iota(iota_tok[:], pattern=[[0, E], [P, NT]], base=0, channel_multiplier=0,
                           allow_small_or_imprecise_dtypes=True).then_inc(masks, 1)
            nc.gpsimd.iota(iota_tile[:], pattern=[[1, ROUNDS * RING], [0, E]], base=0, channel_multiplier=0,
                           allow_small_or_imprecise_dtypes=True).then_inc(masks, 1)
            nc.gpsimd.iota(prefer[:], pattern=[[0, GT], [-1, E]], base=E, channel_multiplier=0,
                           allow_small_or_imprecise_dtypes=True).then_inc(masks, 1)
            nc.gpsimd.iota(counts[:], pattern=[[REGION, E], [0, GT + 1]], base=0, channel_multiplier=0,
                           allow_small_or_imprecise_dtypes=True).then_inc(masks, 1)
            nc.gpsimd.iota(region[:], pattern=[[REGION, E]], base=0, channel_multiplier=0,
                           allow_small_or_imprecise_dtypes=True).then_inc(masks, 1)
            chain.link(nc.gpsimd.memset(minus_half[:], -0.5))
            chain.link(nc.gpsimd.memset(carry[:], 1.0))
            nc.gpsimd.memset(carry[:, :, 0:1], 0.0).then_inc(masks, 1)

            def route_root(r):
                pool.wait_ge(var2_ready, r + 1)
                nc.gpsimd.tensor_tensor(guess2[:], var2[:], minus_half[:], ALU.pow).then_inc(guess2_ready, 1)

            def route_norm(r, par):
                ready = r + 1 if isinstance(r, int) else pool.to_reg(r + 1)
                x1, h2 = row_buf[par][:, :, C:2 * C], row_buf[par][:, :, 0:C]
                pool.wait_ge(masks, 2)
                pool.wait_ge(norm2_ready, ready)
                nc.gpsimd.tensor_tensor(h2, x1, mean2[:].unsqueeze(2).broadcast_to([P, GT, C]), ALU.subtract
                                        ).then_inc(centred, 1)
                pool.wait_ge(masks, 2)
                pool.wait_ge(centred, ready)
                nc.gpsimd.tensor_tensor(h2, h2, rstd2[:].unsqueeze(2).broadcast_to([P, GT, C]), ALU.mult
                                        ).then_inc(plain_ready, 1)

            def route_scatter(r, par):
                there = r + 1 if isinstance(r, int) else pool.to_reg(r + 1)
                pool.wait_ge(masks, 10)
                pool.wait_ge(slots_ready, there)
                for t in range(GT):
                    pool.indirect_dma_start(sorted_rows,
                                            bass.IndirectOffsetOnAxis(ap=slot_i[par][:, t:t + 1], axis=0),
                                            row_buf[par][:, t, :], None).then_inc(scattered[par], 16)

            with pool.Fori(0, G // 2) as k:
                for par in range(2):
                    route_root(2 * k + par)
                    route_norm(2 * k + par, par)
                    route_scatter(2 * k + par, par)

            def rows_out(n, ring):
                ready = n + 1 if isinstance(n, int) else pool.to_reg(n + 1)
                pool.wait_ge(scattered[0], 16 * NT // 2)
                pool.wait_ge(yrow_ready, ready)
                pool.indirect_dma_start(out_rows, bass.IndirectOffsetOnAxis(ap=slot_token[ring][:], axis=0),
                                        y_row[ring], None, bounds_check=B * T - 1, oob_is_err=False
                                        ).then_inc(row_out[ring], 16)

            with pool.Fori(0, ROUNDS - 1) as k:
                for ring in range(RING):
                    rows_out(RING * k + ring, ring)
            for n in range(RING * (ROUNDS - 1), SLOT_TILES):
                rows_out(n, n % RING)

        @blk.scalar
        def _(act):
            act.dma_start(wqkv[:], w_attn).then_inc(wqkv_in, 16)
            act.dma_start(wproj[:], w_proj).then_inc(wproj_in, 16)
            act.dma_start(wg_sb[:], wg).then_inc(wgate_in, 16)
            act.dma_start(bg_row[:], bg.rearrange("(o e) -> o e", o=1)).then_inc(wgate_in, 16)
            chain = Count(act, act_chain)
            act.wait_ge(c_in, 16)
            nc.scalar.activation(c_exp[:], c_col[:], ACT.Exp, scale=-1.0).then_inc(c_exp_done, 1)
            act.wait_ge(var_ready, 1)
            nc.scalar.activation(root[:], var[:], ACT.Sqrt).then_inc(root_ready, 1)
            act.wait_ge(mod_ready, 1)
            act.wait_ge(norm_ready, 1)

            def front_norm(f):
                if not isinstance(f, int) or f:
                    act.wait_ge(xt_mm, f)
                for t in range(GT):
                    n = GT * f + t
                    last = nc.scalar.activation(xhat[:, t:t + 1, :], x_all[:, bass.ds(n, 1), :], ACT.Identity,
                                                bias=shift[:, bass.ds(n, 1)], scale=rstd[:, bass.ds(n, 1)])
                last.then_inc(xhat_ready, 1)

            def front_ht(f):
                act.wait_ge(xt_mm, f + 1)
                for b in range(B):
                    cols = slice(2 * P * b, 2 * P * b + 2 * P)
                    last = nc.scalar.activation(h_t[:, cols], F0[:, cols], ACT.Identity, bias=sa_col[:, b:b + 1],
                                                scale=ca1_col[:, b:b + 1])
                last.then_inc(ht_ready, 1)

            def front_exp(f, chain):
                act.wait_ge(q_mm, f + 1)
                chain.link(nc.scalar.activation(relu_q[:], F1[:], ACT.Relu, scale=-1.0))
                act.wait_ge(q_ready, f)
                nc.scalar.activation(exp_q[:], relu_q[:], ACT.Exp, scale=-1.0).then_inc(eq_ready, 1)
                act.wait_ge(k_mm, f + 1)
                chain.link(nc.scalar.activation(relu_k[:], F2[:], ACT.Relu, scale=-1.0))
                act.wait_ge(k_ready, f)
                nc.scalar.activation(exp_k[:], relu_k[:], ACT.Exp, scale=-1.0).then_inc(ek_ready, 1)

            def masked_q(f, par):
                act.wait_ge(q_ready, f + 1)
                for a in range(QUADS):
                    last = nc.scalar.activation(q_m[par][:, a, :], q_t[par][:], ACT.Copy, scale=quad_head[:, a:a + 1])
                last.then_inc(qm_ready, 1)

            def front_v(f, par):
                act.wait_ge(v_mm, f + 1)
                nc.scalar.activation(v_n[par][:], F0[:], ACT.Copy)
                for t in range(GT):
                    diag = v_m[par][:, t].rearrange("p (a w) -> p a w", w=P + HD)[:, :, 0:P].rearrange(
                        "p a (q r) -> p a q r", q=QUADS)[:, :, :, 0:HD]
                    last = nc.scalar.activation(diag, F0[:, t * P:(t + 1) * P].rearrange(
                        "p (q a j) -> p a q j", q=QUADS, a=QUADS), ACT.Copy)
                last.then_inc(v_ready, 1)
                act.wait_ge(k_ready, f + 1)
                for q in range(QUADS):
                    rows = slice(32 * q, 32 * q + 32)
                    last = nc.scalar.activation(k_q[par][rows, q, :], k_t[par][rows, :], ACT.Copy)
                last.then_inc(kq_ready, 1)

            def front_kn(f, par):
                act.wait_ge(kt_mm, f + 1)
                nc.scalar.activation(k_n[par][:], F1[:], ACT.Copy).then_inc(kn_ready, 1)

            def front_rden(f, par):
                act.wait_ge(inv_mm, f + 1)
                nc.scalar.activation(rden[par][:], F2[:], ACT.Copy).then_inc(rden_ready, 1)

            def route_turned(r):
                act.wait_ge(h2t_mm, r + 1)
                nc.scalar.activation(h2_t[:], F0[:], ACT.Copy).then_inc(h2t_ready, 1)

            def step(g, par, chain, front=True, norm=True, route=True):
                f, fpar = g + 1, 1 - par
                if front:
                    front_ht(f)
                    front_exp(f, chain)
                    front_v(f, fpar)
                    front_kn(f, fpar)
                if route:
                    route_turned(g - 1)
                if front:
                    masked_q(f, fpar)
                    front_rden(f, fpar)
                if norm:
                    front_norm(f + 1)

            front_norm(0)
            front_ht(0)
            front_exp(0, chain)
            act.wait_ge(masks, 7)
            masked_q(0, 0)
            front_v(0, 0)
            front_norm(1)
            front_kn(0, 0)
            front_rden(0, 0)
            step(0, 0, chain, route=False)
            before = chain.n
            with act.Fori(0, G // 2 - 2) as k:
                step(2 * k + 1, 1, Count(act, act_chain, before + 4 * k))
                step(2 * k + 2, 0, Count(act, act_chain, before + 4 * k + 2))
            chain.n = before + 2 * (G - 4)
            step(G - 3, 1, chain)
            step(G - 2, 0, chain, norm=False)
            step(G - 1, 1, None, front=False, norm=False)
            route_turned(G - 1)
            close_runs(act, range(1, E, 2))

            def column(n, par):
                wait_ge(act, up_mm, n - 1)
                act.wait_ge(row_mm, n + 1)
                nc.scalar.activation(h_col[par], [F0, F1][par][:, 0:P], ACT.Copy).then_inc(col_ready, 1)

            def hidden(n, par):
                wait_ge(act, down_mm, n - 1)
                act.wait_ge(up_mm, n + 1)
                nc.scalar.activation(gelu[par], [S0, S1][par][:].rearrange("p (k c) -> p k c", k=HC), ACT.Gelu_apprx_tanh).then_inc(gelu_ready, 1)

            def experts(k, edge):
                for j in range(RING):
                    n = RING * k + j
                    if edge < 1 or n < SLOT_TILES:
                        hidden(n, j % 2)
                    if edge < 1 or n + 2 < SLOT_TILES:
                        column(n + 2, j % 2)

            column(0, 0)
            column(1, 1)
            experts(0, 0)
            with act.Fori(1, ROUNDS - 1) as k:
                experts(k, 0)
            experts(ROUNDS - 1, 1)

        @blk.vector
        def _(dve):
            V = nc.vector
            chain = Count(dve, dve_chain)

            def spread(st, mean, diff, var, chain):
                V.tensor_tensor(diff[:], st[:, :, 1], st[:, :, 4], ALU.subtract)
                V.tensor_tensor(mean[:], st[:, :, 1], st[:, :, 4], ALU.add)
                chain.link(V.tensor_tensor(var[:], st[:, :, 2], st[:, :, 5], ALU.add))
                V.tensor_scalar(mean[:], mean[:], 0.5, None, ALU.mult)
                V.tensor_scalar(var[:], var[:], 1.0 / C, EPS, ALU.mult, ALU.add)
                chain.link(V.tensor_tensor(diff[:], diff[:], diff[:], ALU.mult))
                return V.scalar_tensor_tensor(out=var[:], in0=diff[:], scalar=0.25, in1=var[:], op0=ALU.mult,
                                              op1=ALU.add)

            def newton(rstd, guess, tmp, var, chain):
                chain.link(V.tensor_tensor(tmp[:], guess[:], guess[:], ALU.mult))
                chain.link(V.tensor_tensor(tmp[:], tmp[:], var[:], ALU.mult))
                chain.link(V.tensor_scalar(tmp[:], tmp[:], -0.5, 1.5, ALU.mult, ALU.add))
                return V.tensor_tensor(rstd[:], guess[:], tmp[:], ALU.mult)

            dve.wait_ge(c_exp_done, 1)
            chain.link(V.tensor_scalar(c_exp[:], c_exp[:], 1.0, None, ALU.add))
            chain.link(V.reciprocal(c_exp[:], c_exp[:]))
            chain.link(V.tensor_tensor(c_silu[:], c_col[:], c_exp[:], ALU.mult))
            dve.wait_ge(consts, 2)
            for b in range(B):
                last = V.tensor_scalar(c_bc[:, b, :], ones[:], c_silu[:, b:b + 1], None, ALU.mult)
            last.then_inc(c_ready, 1)
            for g in range(G):
                dve.wait_ge(x_in[g], 32)
                for t in range(GT):
                    last = V.bn_stats(stats[:, GT * g + t, :], x_all[:, GT * g + t, :])
            chain.link(last)
            spread(stats, mean, diff, var, chain).then_inc(var_ready, 1)
            dve.wait_ge(mod_mm, 1)
            V.tensor_copy(sa_col[:], F1[:, 0:B])
            V.tensor_scalar(ca1_col[:], F1[:, B:2 * B], 1.0, None, ALU.add)
            V.tensor_copy(bg_bc[:], F2[:, 0:E])
            for b in range(B):
                last = V.tensor_copy(mod_bc[:, b].rearrange("p k c -> p (k c)"), [S0, S1][b][:])
                last.then_inc(probs_ready, 1)
            dve.wait_ge(probs_ready, 2)
            mod = mod_bc[:]
            gates = mod_bc[:, :, 0:4:3, :]
            for b in range(B):
                gb_in = mod_bc[:, b, 0:4:3, :]
                V.tensor_scalar(gate_s[:, b], gb_in, 0.0, None, ALU.is_ge)
                last = V.tensor_scalar(gate_a[:, b], gb_in, -1.0, None, ALU.mult)
            V.tensor_scalar(mod_bc[:, :, 2, :], mod_bc[:, :, 2, :], 1.0, None, ALU.add)
            chain.link(last)
            for b in range(B):
                last = V.tensor_tensor(gate_a[:, b], gate_a[:, b], mod_bc[:, b, 0:4:3, :], ALU.max)
                V.tensor_scalar(gate_s[:, b], gate_s[:, b], 2.0, -1.0, ALU.mult, ALU.add)
            chain.link(last)
            chain.link(V.tensor_scalar(gate_a[:], gate_a[:], MOD_MIN, None, ALU.max))
            for b in range(B):
                last = V.tensor_tensor(mod_bc[:, b, 0:4:3, :], gate_a[:, b], gate_s[:, b], ALU.mult)
            chain.link(last)
            dve.wait_ge(wproj_in, 16)
            for b in range(B):
                V.tensor_tensor(wproj_b[:, b], wproj[:], mod_bc[:, b, 0], ALU.mult)
            dve.wait_ge(masks, 1)
            V.tensor_reduce(quad_head[:], block[:].rearrange("p (q a j) -> p a q j", q=QUADS, a=QUADS)[:, :, :, 0],
                            AX.X, ALU.add).then_inc(mod_ready, 1)
            V.tensor_tensor(gb_diff[:], mod_bc[:, 1, 3], mod_bc[:, 0, 3], ALU.subtract)
            V.memset(den[:, 0:1], 0.0).then_inc(y_ready, 2)
            V.memset(den[:, 1:2], 0.0).then_inc(x1_ready, 1)

            dve.wait_ge(root_ready, 1)
            chain.link(V.reciprocal(root[:], root[:]))
            chain.link(newton(rstd, root, diff, var, chain))
            V.scalar_tensor_tensor(out=shift[:], in0=mean[:], scalar=-1.0, in1=rstd[:], op0=ALU.mult,
                                   op1=ALU.mult).then_inc(norm_ready, 1)
            dve.wait_ge(masks, 3)

            def front_elu_q(f, par):
                dve.wait_ge(eq_ready, f + 1)
                V.scalar_tensor_tensor(out=q_t[par][:], in0=F1[:], scalar=0.0, in1=exp_q[:], op0=ALU.max,
                                       op1=ALU.add).then_inc(q_ready, 1)

            def front_elu_k(f, par):
                dve.wait_ge(ek_ready, f + 1)
                V.scalar_tensor_tensor(out=k_t[par][:], in0=F2[:], scalar=0.0, in1=exp_k[:], op0=ALU.max,
                                       op1=ALU.add).then_inc(k_ready, 1)

            def front_z(f, par, chain, first=False):
                dve.wait_ge(k_ready, f + 1)
                for b in range(B):
                    cols = slice(2 * P * b, 2 * P * b + 2 * P)
                    start = 0.0 if first else z_t[1 - par][:, 2 * P * b + 2 * P - 1:2 * P * b + 2 * P]
                    last = V.tensor_tensor_scan(z_t[par][:, cols], ones[:, 0:1].broadcast_to([P, 2 * P]),
                                                k_t[par][:, cols], start, ALU.mult, ALU.add)
                chain.link(last)
                V.tensor_tensor(qz[:], z_t[par][:], q_t[par][:], ALU.mult).then_inc(qz_ready, 1)

            def front_rden(f, par, chain):
                dve.wait_ge(den_mm, f + 1)
                chain.link(V.tensor_scalar(den[:], F2[:, 0:GT * HEADS], DEN_EPS, None, ALU.add))
                chain.link(V.reciprocal(den_inv[:], den[:]))
                V.tensor_copy(qz[:].rearrange("p (n j) -> p n j", j=HD),
                              den_inv[:].unsqueeze(2).broadcast_to([P, GT * HEADS, HD])).then_inc(inv_ready, 1)

            def core_probs(g, s, b):
                wait_ge(dve, y_mm, 4 * g + 2 * s - 1)
                for q in range(QUADS):
                    dve.wait_ge(score_mm, 16 * g + 8 * s + 4 * b + q + 1)
                    V.tensor_tensor(probs[:, s, b, q, :], score_bank[q % 2][:, 0:QUADS * L],
                                    causal[:].rearrange("p a t -> p (a t)"), ALU.mult).then_inc(probs_ready, 1)

            def core_state(g, u):
                dve.wait_ge(kv_mm, 4 * g + u + 1)
                V.tensor_tensor(state[:, u % 2], ST[:, 0:2 * P].rearrange("p (b c) -> p b c", b=B),
                                block[:].unsqueeze(1).broadcast_to([P, B, P]), ALU.mult).then_inc(state_ready, 1)

            def core_y(g, par, u):
                s, half = u // 2, u % 2
                if u == 0:
                    dve.wait_ge(rden_ready, g + 1)
                dve.wait_ge(y_mm, 4 * g + u + 2)
                r = rden[par][:].rearrange("p (b s h t) -> p b s h t", b=B, s=2, h=2)[:, :, s, half, :]
                V.tensor_tensor(y_n[:, s, :, L * half:L * half + L],
                                y_bank[half][:, 0:2 * L].rearrange("p (b t) -> p b t", b=B), r,
                                ALU.mult).then_inc(y_ready, 1)

            def core_x1(g, par, turn):
                if par:
                    dve.wait_ge(scattered[1], 16 * GT * turn + 16)
                elif not isinstance(g, int) or g:
                    dve.wait_ge(scattered[0], 16 * GT * turn)
                if not isinstance(g, int) or g:
                    V.tensor_scalar(row_buf[par][:, :, 2 * C], row_buf[par][:, :, 2 * C], 4.0 * P, None, ALU.add)
                dve.wait_ge(proj_mm, g + 1)
                V.tensor_tensor(row_buf[par][:, :, C:2 * C], x_all[:, bass.ds(GT * g, GT), :],
                                F0[:].rearrange("p (t c) -> p t c", t=GT), ALU.add).then_inc(x1_ready, 1)

            def route_stats(r, par, chain):
                dve.wait_ge(x1_ready, r + 2)
                for t in range(GT):
                    last = V.bn_stats(stats2[:, t, :], row_buf[par][:, t, C:2 * C])
                if not isinstance(r, int) or r:
                    dve.wait_ge(plain_ready, r)
                chain.link(last)
                spread(stats2, mean2, diff2, var2, chain).then_inc(var2_ready, 1)

            def route_newton(r, chain):
                dve.wait_ge(guess2_ready, r + 1)
                newton(rstd2, guess2, newton2, var2, chain).then_inc(norm2_ready, 1)

            def route_modulate(r, par, chain):
                dve.wait_ge(plain_ready, r + 1)
                h2 = row_buf[par][:, :, 0:C].rearrange("p (b s) c -> p b s c", b=B)
                chain.link(V.tensor_tensor(h2, h2, mod_bc[:, :, 2, :].unsqueeze(2).broadcast_to([P, B, 2, C]),
                                           ALU.mult))
                V.tensor_tensor(h2, h2, mod_bc[:, :, 1, :].unsqueeze(2).broadcast_to([P, B, 2, C]),
                                ALU.add).then_inc(h2_ready, 1)

            def route_argmax(r, chain):
                dve.wait_ge(logit_mm, r + 1)
                chain.link(V.tensor_tensor(logit[:], LOGIT.rearrange("p (n e) -> p n e", e=E),
                                           bg_bc[:].unsqueeze(1).broadcast_to([P, GT, E]), ALU.add))
                chain.link(V.tensor_reduce(best[:], logit[:], AX.X, ALU.max))
                chain.link(V.tensor_tensor(logit[:], logit[:], best[:].unsqueeze(2).broadcast_to([P, GT, E]),
                                           ALU.is_ge))
                chain.link(V.tensor_tensor(logit[:], logit[:], prefer[:], ALU.mult))
                chain.link(V.tensor_reduce(best[:], logit[:], AX.X, ALU.max))
                V.tensor_tensor(onehot[:], logit[:], best[:].unsqueeze(2).broadcast_to([P, GT, E]),
                                ALU.is_equal).then_inc(onehot_ready, 1)

            def route_slots(r, par, chain):
                dve.wait_ge(rank_mm, r + 1)
                chain.link(V.tensor_copy(counts[:, :, 1:GT + 1], TOTAL.rearrange("p (n e) -> p e n", e=E)))
                chain.link(V.tensor_tensor_scan(place[:].rearrange("p e n -> p (e n)"),
                                                carry[:].rearrange("p e n -> p (e n)"),
                                                counts[:].rearrange("p e n -> p (e n)"), 0.0, ALU.mult, ALU.add))
                V.tensor_copy(counts[:, :, 0:1], place[:, :, GT:GT + 1])
                chain.link(V.tensor_tensor(pick_row[:], RANK.rearrange("p (n e) -> p n e", e=E),
                                           place[:, :, 0:GT].rearrange("p e n -> p n e"), ALU.add))
                chain.link(V.tensor_tensor(pick_row[:], pick_row[:], onehot[:], ALU.mult))
                chain.link(V.tensor_reduce(slot_f[:], pick_row[:], AX.X, ALU.add))
                V.tensor_copy(slot_i[par][:], slot_f[:]).then_inc(slots_ready, 1)

            LINKS = 3 + 3 + 1 + 5 + 5 + 1 + 2

            def step(g, par, turn, chain, front=True, route=True):
                f, fpar = g + 1, 1 - par
                n = chain.n
                core_probs(g, 0, 1)
                if route:
                    route_stats(g - 1, 1 - par, chain)
                core_y(g, par, 0)
                if front:
                    front_elu_q(f, fpar)
                if route:
                    route_newton(g - 1, chain)
                if front:
                    front_elu_k(f, fpar)
                core_state(g, 2)
                core_probs(g, 1, 0)
                core_y(g, par, 1)
                if route:
                    route_modulate(g - 1, 1 - par, chain)
                core_state(g, 3)
                core_probs(g, 1, 1)
                if front:
                    front_z(f, fpar, chain)
                if route:
                    route_argmax(g - 1, chain)
                core_y(g, par, 2)
                if front:
                    front_rden(f, fpar, chain)
                if route:
                    route_slots(g - 1, 1 - par, chain)
                if front:
                    core_state(g, 4)
                    core_probs(f, 0, 0)
                core_y(g, par, 3)
                if front:
                    core_state(f, 1)
                core_x1(g, par, turn)
                if front and route:
                    assert chain.n - n == LINKS, chain.n - n

            front_elu_q(0, 0)
            front_elu_k(0, 0)
            front_z(0, 0, chain, True)
            front_rden(0, 0, chain)
            core_state(0, 0)
            core_probs(0, 0, 0)
            core_state(0, 1)
            step(0, 0, 0, chain, route=False)
            dve.wait_ge(masks, 13)
            before = chain.n
            with dve.Fori(0, G // 2 - 1) as k:
                step(2 * k + 1, 1, k, Count(dve, dve_chain, before + 2 * LINKS * k))
                step(2 * k + 2, 0, k + 1, Count(dve, dve_chain, before + 2 * LINKS * k + LINKS))
            chain.n = before + LINKS * (G - 2)
            step(G - 1, 1, G // 2 - 1, chain, front=False)
            route_stats(G - 1, 1, chain)
            route_newton(G - 1, chain)
            route_modulate(G - 1, 1, chain)
            route_argmax(G - 1, chain)
            route_slots(G - 1, 1, chain)

            V.tensor_copy(tail_i[:], place[0:1, :, GT]).then_inc(tails_ready, 1)
            chain.link(V.tensor_tensor(cnt[:], place[0:1, :, GT], region[:], ALU.subtract))
            chain.link(V.tensor_tensor(r_cmp[:], cnt[:].unsqueeze(2).broadcast_to([1, E, NT]), iota_tok[:], ALU.is_gt))
            chain.link(V.tensor_reduce(tiles_e[:], r_cmp[:], AX.X, ALU.add))
            chain.link(V.tensor_tensor_scan(tiles_cum[:], ones[0:1, 0:1].broadcast_to([1, E]), tiles_e[:], 0.0,
                                            ALU.mult, ALU.add))
            V.tensor_scalar(tiles_e[:], tiles_e[:], -1.0, float(EXPERT_TILES), ALU.mult, ALU.add)
            chain.link(V.tensor_tensor(t_cmp[:], tiles_cum[:].unsqueeze(1).broadcast_to([1, ROUNDS * RING, E]),
                                       iota_tile[:], ALU.is_le))
            V.tensor_reduce(t_exp[:], t_cmp[:], AX.X, ALU.add)
            chain.link(V.tensor_tensor(t_skip[:], t_cmp[:], tiles_e[:].unsqueeze(1).broadcast_to(
                [1, ROUNDS * RING, E]), ALU.mult))
            V.tensor_scalar(t_exp[:], t_exp[:], float(E - 1), None, ALU.min)
            chain.link(V.tensor_reduce(t_row[:], t_skip[:], AX.X, ALU.add))
            chain.link(V.tensor_tensor(t_row[:], t_row[:], iota_tile[:, :, 0], ALU.add))
            chain.link(V.tensor_scalar(t_row[:], t_row[:], float(E * EXPERT_TILES), None, ALU.min))
            V.tensor_copy(t_row_i[:], t_row[:]).then_inc(table_ready, 1)
            t_ring = t_exp[:].rearrange("o (n r) -> o n r", r=RING)
            chain.link(V.scalar_tensor_tensor(out=code[:], in0=t_ring[:, :, RING - 1], scalar=float(E),
                                              in1=t_ring[:, :, RING - 2],
                                              op0=ALU.mult, op1=ALU.add))
            for j in range(RING - 3, -1, -1):
                chain.link(V.scalar_tensor_tensor(out=code[:], in0=code[:], scalar=float(E), in1=t_ring[:, :, j],
                                                  op0=ALU.mult, op1=ALU.add))
            chain.link(V.tensor_copy(t_code[:], code[:]))

            dve.wait_ge(w1_in, 16)
            dve.wait_ge(w2_in, 16)

            def pick_w1(n, wbuf, code, j):
                wait_ge(dve, up_mm, n - WBUFS + 1)
                V.tensor_copy(w1_cur[wbuf], w1_all[:, bass.ds((code >> (3 * j)) & (E - 1), 1)].rearrange(
                    "p o h -> p (o h)")).then_inc(w1c_ready, 1)

            def pick_w2(n, wbuf, code, j):
                wait_ge(dve, down_mm, n - WBUFS + 1)
                V.tensor_copy(w2_cur[wbuf], w2_all[:, bass.ds((code >> (3 * j)) & (E - 1), 1)].rearrange(
                    "p o k c -> p (o k) c")).then_inc(w2c_ready, 1)

            def finish(n, par, ring, k):
                row = slot_row[ring]
                wait_ge(dve, row_in[ring], 16 * k + 16)
                V.scalar_tensor_tensor(out=gb_sel[par], in0=gb_diff[:], scalar=row[:, 2 * C + 1:2 * C + 2],
                                       in1=mod_bc[:, 0, 3], op0=ALU.mult, op1=ALU.add).then_inc(gated_ready, 1)
                wait_ge(dve, row_out[ring], 16 * k)
                V.tensor_scalar(slot_token[ring][:], row[:, 2 * C:2 * C + 1], float(NO_TOKEN), None, ALU.add)
                dve.wait_ge(down_mm, n + 1)
                dve.wait_ge(gated_ready, 2 * n + 1)
                V.tensor_tensor(y_gated[par], [Y0, Y1][par][:, 0:C], gb_sel[par], ALU.mult
                                ).then_inc(gated_ready, 1)
                dve.wait_ge(gated_ready, 2 * n + 2)
                V.tensor_tensor(y_row[ring], y_gated[par], row[:, C:2 * C], ALU.add).then_inc(yrow_ready, 1)

            def experts(k, edge):
                code = dve.value_load(t_code[0:1, bass.ds(k, 1)] if not isinstance(k, int) else t_code[0:1, k:k + 1],
                                      min_val=0, max_val=E ** RING - 1)
                for j in range(RING):
                    n = RING * k + j
                    there = not edge or n < SLOT_TILES
                    if there:
                        pick_w1(n, j % WBUFS, code, j)
                        pick_w2(n, j % WBUFS, code, j)
                    if not isinstance(n, int) or 3 <= n < SLOT_TILES + 3:
                        finish(n - 3, (j + 1) % 2, (j - 3) % RING, k if j >= 3 else k - 1)

            experts(0, False)
            with dve.Fori(1, ROUNDS - 1) as k:
                experts(k, False)
            experts(ROUNDS - 1, True)
            for n in range(RING * ROUNDS - 3, SLOT_TILES):
                finish(n, n % 2, n % RING, ROUNDS - 1)

        @blk.tensor
        def _(pe):
            mm = nc.tensor.matmul
            pe.wait_ge(c_ready, 1)
            pe.wait_ge(wmod_in, 16)
            pe.wait_ge(wgate_in, 32)
            pe.wait_ge(consts, 2)
            for k in range(2):
                mm(F1[:, B * k:B * k + B], wmod_sb[:, k * C:(k + 1) * C], c_silu[:], start=True, stop=True)
            mm(F2[:, 0:E], ones[0:1, :], bg_row[:], start=True, stop=True)
            for b in range(B):
                mm([S0, S1][b][:], c_bc[:, b, :], wmod_sb[:, 2 * C:6 * C], start=True, stop=True)
            pe.wait_ge(pool_chain, 1)
            mm(ST[:, 0:2 * P], zeros[:, 0:P], zeros[:, 0:2 * P], start=True, stop=True).then_inc(kv_mm, 1)
            mm(ST[:, 0:P], zeros[:, 0:P], zeros[:, 0:P], start=False, stop=True,
               skip_group_check=True).then_inc(y_mm, 1)
            mm(ST[:, 0:2 * P], zeros[:, 0:P], zeros[:, 0:2 * P], start=False, stop=True,
               skip_group_check=True).then_inc(mod_mm, 1)
            pe.wait_ge(wqkv_in, 16)

            def front_x(f):
                pe.wait_ge(xhat_ready, f + 1)
                pe.wait_ge(v_ready, f)
                if not isinstance(f, int) or f >= 1:
                    pe.wait_ge(x1_ready, f)
                for t in range(GT):
                    last = nc.tensor.transpose(F0[:, t * P:(t + 1) * P], xhat[:, t, :], ident[:])
                last.then_inc(xt_mm, 1)

            def front_qkv(f):
                pe.wait_ge(ht_ready, f + 1)
                pe.wait_ge(kn_ready, f)
                mm(F1[:], wqkv[:, 0:C], h_t[:], start=True, stop=True).then_inc(q_mm, 1)
                pe.wait_ge(rden_ready, f)
                mm(F2[:], wqkv[:, C:2 * C], h_t[:], start=True, stop=True).then_inc(k_mm, 1)
                for t in range(GT):
                    last = mm(F0[:, t * P:(t + 1) * P], h_t[:, t * P:(t + 1) * P], wqkv[:, 2 * C:3 * C],
                              start=True, stop=True)
                last.then_inc(v_mm, 1)

            def front_kt(f, par):
                pe.wait_ge(k_ready, f + 1)
                for t in range(GT):
                    last = nc.tensor.transpose(F1[:, t * P:(t + 1) * P], k_t[par][:, t * P:(t + 1) * P], ident[:])
                last.then_inc(kt_mm, 1)

            def front_den(f):
                pe.wait_ge(qz_ready, f + 1)
                for t in range(GT):
                    last = mm(F2[:, HEADS * t:HEADS * t + HEADS], qz[:, t * P:(t + 1) * P],
                              block[:].rearrange("p (h j) -> p h j", j=HD)[:, :, 0], start=True, stop=True)
                last.then_inc(den_mm, 1)

            def front_inv(f):
                pe.wait_ge(inv_ready, f + 1)
                for t in range(GT):
                    last = nc.tensor.transpose(F2[:, t * P:(t + 1) * P], qz[:, t * P:(t + 1) * P], ident[:])
                last.then_inc(inv_mm, 1)

            def core_scores(g, par, s, b):
                t = 2 * b + s
                if s == 0 and b == 0:
                    pe.wait_ge(qm_ready, g + 1)
                    pe.wait_ge(kq_ready, g + 1)
                for q in range(QUADS):
                    pe.wait_ge(probs_ready, 16 * g + 8 * s + 4 * b + q + 1)
                    for half in range(2):
                        tok = t * P + half * L
                        last = mm(score_bank[q % 2][L * half:L * half + L, 0:QUADS * L], k_q[par][:, q, tok:tok + L],
                                  q_m[par][:, :, tok:tok + L], start=True, stop=True)
                    last.then_inc(score_mm, 1)

            def core_across(g, par, u):
                s, half = u // 2, u % 2
                pe.wait_ge(state_ready, 4 * g + u + 1)
                pe.wait_ge(y_ready, 4 * g + u + 1)
                for b in range(B):
                    tok = (2 * b + s) * P + half * L
                    mm(y_bank[half][:, b * L:b * L + L], state[:, half, b, :], q_t[par][:, tok:tok + L],
                       start=(b == 0), stop=False, skip_group_check=True)
                if u == 0:
                    pe.wait_ge(kn_ready, g + 1)
                    pe.wait_ge(v_ready, g + 1)
                rows = slice(L * half, L * half + L)
                for b in range(B):
                    last = mm(ST[:, b * P:(b + 1) * P], k_n[par][rows, 2 * b + s, :], v_n[par][rows, 2 * b + s, :],
                              start=False, stop=True, skip_group_check=True)
                last.then_inc(kv_mm, 1)

            def core_within(g, par, u):
                s, half = u // 2, u % 2
                masked = 2 + 16 * g + 8 * s + 8
                masked = masked if isinstance(masked, int) else pe.to_reg(masked)
                pe.wait_ge(masks, 5)
                pe.wait_ge(probs_ready, masked)
                rows = slice(L * half, L * half + L)
                for b in range(B):
                    for a in range(QUADS):
                        for q in range(QUADS):
                            last = mm(y_bank[half][32 * q:32 * q + 32, b * L:b * L + L],
                                      v_m[par][rows, 2 * b + s, C * a + 32 * q:C * a + 32 * q + 32],
                                      probs[rows, s, b, q, a * L:a * L + L], start=False, stop=(a == QUADS - 1),
                                      skip_group_check=True)
                last.then_inc(y_mm, 1)

            def core_proj(g, front, route):
                if route:
                    pe.wait_ge(slots_ready, g)
                elif front:
                    pe.wait_ge(v_ready, g + 2)
                pe.wait_ge(y_ready, 2 + 4 * g + 4)
                for t in range(GT):
                    last = mm(F0[:, t * P:(t + 1) * P], y_n[:, t % 2, t // 2, :], wproj_b[:, t // 2, :],
                              start=True, stop=True)
                last.then_inc(proj_mm, 1)

            def route_turn(r, par, front=False):
                pe.wait_ge(h2_ready, r + 1)
                if front:
                    pe.wait_ge(v_ready, r + 3)
                for t in range(GT):
                    last = nc.tensor.transpose(F0[:, t * P:(t + 1) * P], row_buf[par][:, t, 0:C], ident[:])
                last.then_inc(h2t_mm, 1)

            def route_logits(r):
                pe.wait_ge(h2t_ready, r + 1)
                for t in range(GT):
                    last = mm(LOGIT[:, t * E:(t + 1) * E], h2_t[:, t * P:(t + 1) * P], wg_sb[:],
                              start=True, stop=True)
                last.then_inc(logit_mm, 1)

            def route_rank(r):
                pe.wait_ge(onehot_ready, r + 1)
                hot = onehot[:].rearrange("p n e -> p (n e)")
                mm(RANK, upper[:], hot, start=True, stop=True)
                mm(TOTAL, ones[:], hot, start=True, stop=True).then_inc(rank_mm, 1)

            def step(g, par, front=True, route=True):
                f, fpar = g + 1, 1 - par
                core_scores(g, par, 0, 1)
                if front:
                    front_x(f)
                core_within(g, par, 0)
                if front:
                    front_qkv(f)
                core_across(g, par, 1)
                core_scores(g, par, 1, 0)
                core_within(g, par, 1)
                if front:
                    front_kt(f, fpar)
                core_across(g, par, 2)
                if route:
                    route_turn(g - 1, 1 - par, front)
                core_scores(g, par, 1, 1)
                if route:
                    route_logits(g - 1)
                core_within(g, par, 2)
                if front:
                    front_den(f)
                core_across(g, par, 3)
                if route:
                    route_rank(g - 1)
                if front:
                    front_inv(f)
                    core_scores(f, fpar, 0, 0)
                core_within(g, par, 3)
                if front:
                    core_across(f, fpar, 0)
                core_proj(g, front, route)

            front_x(0)
            front_qkv(0)
            front_kt(0, 0)
            front_den(0)
            front_inv(0)
            core_scores(0, 0, 0, 0)
            core_across(0, 0, 0)
            step(0, 0, route=False)
            with pe.Fori(0, G // 2 - 1) as k:
                step(2 * k + 1, 1)
                step(2 * k + 2, 0)
            step(G - 1, 1, front=False)
            route_turn(G - 1, 1)
            route_logits(G - 1)
            route_rank(G - 1)
            pe.wait_ge(slots_ready, G)

            def expert_turn(n, ring, k):
                pe.wait_ge(row_in[ring], 16 * k + 16)
                wait_ge(pe, col_ready, n - 1)
                nc.tensor.transpose([F0, F1][ring % 2][:, 0:P], slot_row[ring][:, 0:C], ident[:]).then_inc(row_mm, 1)

            def expert_up(n, par, wbuf):
                pe.wait_ge(w1c_ready, n + 1)
                pe.wait_ge(col_ready, n + 1)
                wait_ge(pe, gelu_ready, n - 1)
                for j in range(HC):
                    last = mm([S0, S1][par][:, j * P:(j + 1) * P], w1_cur[wbuf][:, j * P:(j + 1) * P], h_col[par],
                              start=True, stop=True)
                last.then_inc(up_mm, 1)

            def expert_down(n, par, wbuf):
                pe.wait_ge(gelu_ready, n + 1)
                pe.wait_ge(w2c_ready, n + 1)
                wait_ge(pe, gated_ready, 2 * n - 2)
                for j in range(HC):
                    last = mm([Y0, Y1][par][:, 0:C], gelu[par][:, j, :], w2_cur[wbuf][:, j, :], start=(j == 0),
                              stop=(j == HC - 1))
                last.then_inc(down_mm, 1)

            def experts(k, edge):
                for j in range(RING):
                    n = RING * k + j
                    if not edge or n + 2 < SLOT_TILES:
                        expert_turn(n + 2, (j + 2) % RING, k + (j + 2) // RING)
                    if not edge or n + 1 < SLOT_TILES:
                        expert_up(n + 1, (j + 1) % 2, (j + 1) % WBUFS)
                    if not edge or n < SLOT_TILES:
                        expert_down(n, j % 2, j % WBUFS)

            expert_turn(0, 0, 0)
            expert_turn(1, 1, 0)
            expert_up(0, 0, 0)
            experts(0, False)
            with pe.Fori(1, ROUNDS - 1) as k:
                experts(k, False)
            experts(ROUNDS - 1, True)


_INS = ['L0_attn_x', 'L0_attn_w_attn', 'L0_attn_w_proj', 'L0_ffn_W1', 'L0_ffn_W2', 'L0_ffn_Wg', 'L0_ffn_bg', 'L0_c',
        'L0_wmod']
_OUTS = [((2, 2048, 128), 'float32')]


def kernel(**inputs):
    import numpy as _np
    import concourse.bacc as _bacc
    from concourse import mybir as _mybir
    from concourse.bass_utils import run_bass_kernel_spmd as _run

    nc = _bacc.Bacc("TRN2", target_bir_lowering=False, num_devices=1)
    arrays, args = {}, []
    for name in _INS:
        a = _np.ascontiguousarray(inputs[name])
        arrays[f"in_{name}_dram"] = a
        args.append(nc.dram_tensor(f"in_{name}_dram", a.shape, _mybir.dt.from_np(a.dtype), kind="ExternalInput").ap())
    for i, (shape, dtype) in enumerate(_OUTS):
        dt = _mybir.dt.from_np(_np.dtype(dtype))
        args.append(nc.dram_tensor(f"out_{i}_dram", shape, dt, kind="ExternalOutput").ap())
    build(nc, *args)
    r = _run(nc, [arrays], core_ids=[0])
    got = tuple(r.results[0][f"out_{i}_dram"] for i in range(len(_OUTS)))
    return got[0]
```

```python
from contextlib import ExitStack

import concourse.bass as bass
from concourse import mybir

F32 = mybir.dt.float32
I32 = mybir.dt.int32
ALU = mybir.AluOpType
ACT = mybir.ActivationFunctionType
AX = mybir.AxisListType

B, T, C = 2, 2048, 128
HEADS, HD = 16, 8
E, HID = 8, 512
P = 128
NT = B * T // P
GT = 4
HEAD, TAIL = slice(0, 2 * GT), slice(2 * GT, NT)
FIRST, LAST = (0, 1), (2, 3)
G = NT // GT
L = 64
HC = HID // P
SLOT_TILES = NT + E - 1
EXPERT_TILES = NT + 1
REGION = EXPERT_TILES * P
CHUNKS = GT * P // L
QUADS = 4
ROW = 2 * C + 8
NO_TOKEN = 8192
RING = 6
WBUFS = 3
ROUNDS = -(-SLOT_TILES // RING)
EPS = 1e-5
DEN_EPS = 1e-6
MOD_MIN = 0.25


def wait_ge(eng, sem, value):
    if not isinstance(value, int) or value > 0:
        eng.wait_ge(sem, value)


class Count:

    def __init__(self, eng, sem, before=0):
        self.eng, self.sem, self.before, self.n = eng, sem, before, 0

    def link(self, *instructions):
        for ins in instructions:
            if ins is not None:
                self.n += 1
                ins.then_inc(self.sem, 1)
        self.eng.wait_ge(self.sem, self.before + self.n)


def build(nc, x, w_attn, w_proj, w1, w2, wg, bg, c, wmod, out):
    sorted_rows = nc.dram_tensor("sorted_rows", ((E * EXPERT_TILES + 1) * P, ROW), F32, kind="Internal").ap()

    with ExitStack() as ctx:
        def sb(name, shape, dt=F32):
            return ctx.enter_context(nc.sbuf_tensor(name, shape, dt))

        def sem(name):
            return ctx.enter_context(nc.semaphore(name))

        x_all = sb("x_all", [P, NT, C])
        row_buf = [sb(f"row_buf{n}", [P, GT, ROW]) for n in range(2)]
        w1_all = sb("w1_all", [P, E, HID])
        w2_all = sb("w2_all", [P, E, HC, C])
        wqkv = sb("wqkv", [P, 3 * C])
        wproj = sb("wproj", [P, C])
        wproj_b = sb("wproj_b", [P, B, C])
        wg_sb = sb("wg_sb", [P, E])
        bg_row = sb("bg_row", [1, E])
        bg_bc = sb("bg_bc", [P, E])
        wmod_sb = sb("wmod_sb", [P, 6 * C])
        c_col = sb("c_col", [P, B])
        c_exp = sb("c_exp", [P, B])
        c_silu = sb("c_silu", [P, B])
        c_bc = sb("c_bc", [P, B, P])
        sa_col = sb("sa_col", [P, B])
        ca1_col = sb("ca1_col", [P, B])
        mod_bc = sb("mod_bc", [P, B, 4, C])
        gate_a = sb("gate_a", [P, B, 2, C])
        gate_s = sb("gate_s", [P, B, 2, C])
        ident = sb("ident", [P, P])
        ones = sb("ones", [P, P])
        zeros = sb("zeros", [P, ROW])
        upper = sb("upper", [P, P])
        block = sb("block", [P, P])
        block_b = sb("block_b", [P, B, P])
        quad_head = sb("quad_head", [P, QUADS])
        causal = sb("causal", [P, QUADS, L])
        iota_tok = sb("iota_tok", [1, E, NT])
        iota_tile = sb("iota_tile", [1, ROUNDS * RING, E])
        prefer = sb("prefer", [P, GT, E])
        stats = sb("stats", [P, NT, 6])
        mean = sb("mean", [P, NT])
        var = sb("var", [P, NT])
        diff = sb("diff", [P, NT])
        root = sb("root", [P, NT])
        rstd, shift = sb("rstd", [P, NT]), sb("shift", [P, NT])
        minus_half = sb("minus_half", [P, GT])
        stats2 = sb("stats2", [P, GT, 6])
        mean2, diff2, var2, guess2, newton2, rstd2 = (
            sb(n, [P, GT]) for n in ("mean2", "diff2", "var2", "guess2", "newton2", "rstd2"))
        xhat = sb("xhat", [P, GT, C])
        h_t = sb("h_t", [P, GT * P])
        relu_q = sb("relu_q", [P, GT * P])
        relu_k = sb("relu_k", [P, GT * P])
        exp_q = sb("exp_q", [P, GT * P])
        exp_k = sb("exp_k", [P, GT * P])
        q_t = [sb(f"q_t{n}", [P, GT * P]) for n in range(2)]
        k_t = [sb(f"k_t{n}", [P, GT * P]) for n in range(2)]
        k_q = [sb(f"k_q{n}", [P, QUADS, GT * P]) for n in range(2)]
        q_m = [sb(f"q_m{n}", [P, QUADS, GT * P]) for n in range(2)]
        k_n = [sb(f"k_n{n}", [P, CHUNKS, C]) for n in range(2)]
        v_n = [sb(f"v_n{n}", [P, CHUNKS, L]) for n in range(2)]
        v_m = [sb(f"v_m{n}", [P, CHUNKS, 2, C]) for n in range(2)]
        z_t = [sb(f"z_t{n}", [P, GT * P]) for n in range(2)]
        qz = sb("qz", [P, GT * P])
        den = sb("den", [P, GT * HEADS])
        den_inv = sb("den_inv", [P, GT * HEADS])
        rden = [sb(f"rden{n}", [P, GT * P]) for n in range(2)]
        probs = sb("probs", [P, 2, B, QUADS, QUADS * L])
        state = sb("state", [P, 2, B, C])
        y_n = sb("y_n", [P, 2, B, P])
        h2_t = sb("h2_t", [P, GT * P])
        logit = sb("logit", [P, GT, E])
        best = sb("best", [P, GT])
        onehot = sb("onehot", [P, GT, E])
        counts = sb("counts", [P, E, GT + 1])
        carry = sb("carry", [P, E, GT + 1])
        place = sb("place", [P, E, GT + 1])
        pick_row = sb("pick_row", [P, GT, E])
        slot_f = sb("slot_f", [P, GT])
        slot_i = [sb(f"slot_i{n}", [P, GT], I32) for n in range(2)]
        region = sb("region", [1, E])
        tail_i = sb("tail_i", [1, E], I32)
        cnt = sb("cnt", [1, E])
        r_cmp = sb("r_cmp", [1, E, NT])
        tiles_e = sb("tiles_e", [1, E])
        tiles_cum = sb("tiles_cum", [1, E])
        t_cmp = sb("t_cmp", [1, ROUNDS * RING, E])
        t_skip = sb("t_skip", [1, ROUNDS * RING, E])
        t_exp = sb("t_exp", [1, ROUNDS * RING])
        t_row = sb("t_row", [1, ROUNDS * RING])
        code = sb("code", [1, ROUNDS])
        t_row_i = sb("t_row_i", [1, ROUNDS * RING], I32)
        t_code = sb("t_code", [1, ROUNDS], I32)
        flat_v = [v_m[n][:].rearrange("p n a c -> p (n a c)") for n in range(2)]
        slot_row = [flat_v[0][:, n * ROW:(n + 1) * ROW] for n in range(RING)]
        gelu = [flat_v[1][:, n * HID:(n + 1) * HID].rearrange("p (k c) -> p k c", k=HC) for n in range(2)]
        flat_q = [q_m[n][:].rearrange("p a t -> p (a t)") for n in range(2)]
        y_row = [flat_q[0][:, n * C:(n + 1) * C] for n in range(RING)]
        gb_sel, y_gated, h_col = ([flat_q[1][:, (2 * i + n) * P:(2 * i + n + 1) * P] for n in range(2)]
                                  for i in range(3))
        w1_cur = [k_q[0][:, n, :] for n in range(WBUFS)]
        w2_cur = [k_q[1][:, n, :].rearrange("p (k c) -> p k c", k=HC) for n in range(WBUFS)]
        slot_token = [sb(f"slot_token{n}", [P, 1], I32) for n in range(RING)]
        gb_diff = sb("gb_diff", [P, C])

        bank = [ctx.enter_context(nc.psum_tensor(f"bank{n}", [P, 512], F32)) for n in range(8)]
        F0, F1, F2, S0, S1, ST, Y0, Y1 = bank
        score_bank, y_bank = [S0, S1], [Y0, Y1]
        LOGIT, RANK, TOTAL = (F0[:, i * GT * E:(i + 1) * GT * E] for i in range(3))

        x_in = [sem(f"x_in{g}") for g in range(G)]
        c_in, wmod_in, wqkv_in, wproj_in, wgate_in, w1_in, w2_in = (
            sem(n) for n in ("c_in", "wmod_in", "wqkv_in", "wproj_in", "wgate_in", "w1_in", "w2_in"))
        consts, masks = sem("consts"), sem("masks")
        c_exp_done, c_ready, cols_mm, mod_mm, quad_ready, mod_out, gate_chain, gates_ready = (
            sem(n) for n in ("c_exp_done", "c_ready", "cols_mm", "mod_mm", "quad_ready", "mod_out", "gate_chain",
                             "gates_ready"))
        var_ready, root_ready, norm_ready = sem("var_ready"), sem("root_ready"), sem("norm_ready")
        dve_chain, act_chain, pool_chain = sem("dve_chain"), sem("act_chain"), sem("pool_chain")
        xhat_ready, xt_mm, ht_ready = sem("xhat_ready"), sem("xt_mm"), sem("ht_ready")
        q_mm, k_mm, v_mm, kt_mm, den_mm = (sem(n) for n in ("q_mm", "k_mm", "v_mm", "kt_mm", "den_mm"))
        eq_ready, ek_ready, q_ready, k_ready, qm_ready = (
            sem(n) for n in ("eq_ready", "ek_ready", "q_ready", "k_ready", "qm_ready"))
        v_ready, kn_ready, kq_ready, qz_ready, inv_ready, inv_mm, rden_ready = (
            sem(n) for n in ("v_ready", "kn_ready", "kq_ready", "qz_ready", "inv_ready", "inv_mm", "rden_ready"))
        score_mm, probs_ready = sem("score_mm"), sem("probs_ready")
        kv_mm, state_ready, y_mm, y_ready = (sem(n) for n in ("kv_mm", "state_ready", "y_mm", "y_ready"))
        proj_mm, x1_ready = sem("proj_mm"), sem("x1_ready")
        var2_ready, guess2_ready, norm2_ready, centred, plain_ready = (
            sem(n) for n in ("var2_ready", "guess2_ready", "norm2_ready", "centred", "plain_ready"))
        h2_ready, h2t_mm, h2t_ready, logit_mm, onehot_ready, rank_mm, slots_ready = (
            sem(n) for n in ("h2_ready", "h2t_mm", "h2t_ready", "logit_mm", "onehot_ready", "rank_mm",
                             "slots_ready"))
        scattered = [sem(f"scattered{n}") for n in range(2)]
        tails_ready, table_ready, closed = sem("tails_ready"), sem("table_ready"), sem("closed")
        row_in = [sem(f"row_in{n}") for n in range(RING)]
        row_mm, col_ready, w1c_ready, w2c_ready, up_mm, gelu_ready, down_mm, gated_ready, yrow_ready = (
            sem(n) for n in ("row_mm", "col_ready", "w1c_ready", "w2c_ready", "up_mm", "gelu_ready", "down_mm",
                             "gated_ready", "yrow_ready"))
        row_out = [sem(f"row_out{n}") for n in range(RING)]

        def close_runs(eng, queue_experts):
            eng.wait_ge(tails_ready, 1)
            for e in queue_experts:
                row = eng.value_load(tail_i[0:1, e:e + 1], min_val=e * REGION, max_val=e * REGION + NT * P)
                eng.dma_start(sorted_rows[bass.ds(row, P)], zeros[:]).then_inc(closed, 16)

        x_v = x.rearrange("b (g s p) c -> b g p s c", s=2, p=P)
        out_rows = out.rearrange("b t c -> (b t) c")
        sorted_v = sorted_rows.rearrange("(n p) c -> n p c", p=P)

        blk = ctx.enter_context(nc.Block())

        @blk.sync
        def _(sp):
            with nc.allow_non_contiguous_dma(reason="256 values of c, by column"):
                sp.dma_start(c_col[:], c.rearrange("b c -> c b")).then_inc(c_in, 16)
            sp.dma_start(wmod_sb[:], wmod).then_inc(wmod_in, 16)
            for g in range(G):
                for b in range(B):
                    sp.dma_start(x_all[:, GT * g + 2 * b:GT * g + 2 * b + 2, :], x_v[b, g]).then_inc(x_in[g], 16)
            sp.dma_start(w1_all[:], w1.rearrange("e d h -> d e h")).then_inc(w1_in, 16)
            sp.dma_start(w2_all[:], w2.rearrange("e (k p) d -> p e k d", p=P)).then_inc(w2_in, 16)

            close_runs(sp, range(0, E, 2))

            sp.wait_ge(table_ready, 1)
            def load(n, ring):
                tile = sp.value_load(t_row_i[0:1, n:n + 1] if isinstance(n, int) else t_row_i[0:1, bass.ds(n, 1)],
                                     min_val=0, max_val=E * EXPERT_TILES)
                if isinstance(n, int) and n == 0:
                    sp.wait_ge(closed, 16 * E)
                    for half in range(2):
                        sp.wait_ge(scattered[half], 16 * (NT // 2 + half))
                wait_ge(sp, yrow_ready, n - RING + 1)
                sp.dma_start(slot_row[ring], sorted_v[bass.ds(tile, 1)].rearrange("o p c -> p (o c)")
                             ).then_inc(row_in[ring], 16)

            for ring in range(RING):
                load(ring, ring)
            with sp.Fori(1, ROUNDS - 1) as k:
                for ring in range(RING):
                    load(RING * k + ring, ring)
            for n in range(RING * (ROUNDS - 1), SLOT_TILES):
                load(n, n % RING)
            for ring in range(RING):
                sp.wait_ge(row_out[ring], 16 * len(range(ring, SLOT_TILES, RING)))

        @blk.gpsimd
        def _(pool):
            chain = Count(pool, pool_chain)
            chain.link(nc.gpsimd.memset(zeros[:], 0.0))
            pool.dma_start(sorted_v[E * EXPERT_TILES], zeros[:]).then_inc(scattered[1], 16)
            chain.link(nc.gpsimd.memset(ident[:], 0.0))
            nc.gpsimd.affine_select(out=ident[:], in_=ident[:], compare_op=ALU.not_equal, fill=1.0, base=0,
                                    pattern=[[-1, P]], channel_multiplier=1).then_inc(consts, 1)
            chain.link(nc.gpsimd.memset(ones[:], 1.0))
            nc.gpsimd.affine_select(out=upper[:], in_=ones[:], compare_op=ALU.is_gt, fill=0.0, base=0,
                                    pattern=[[1, P]], channel_multiplier=-1).then_inc(consts, 1)
            bl = block[:].rearrange("p (h j) -> p h j", j=HD)
            chain.link(nc.gpsimd.affine_select(out=bl, in_=ones[:].rearrange("p (h j) -> p h j", j=HD),
                                               compare_op=ALU.is_ge, fill=0.0, base=0,
                                               pattern=[[-HD, HEADS], [0, HD]], channel_multiplier=1))
            nc.gpsimd.affine_select(out=bl, in_=bl, compare_op=ALU.is_ge, fill=0.0, base=HD - 1,
                                    pattern=[[HD, HEADS], [0, HD]], channel_multiplier=-1).then_inc(masks, 1)
            chain.link(nc.gpsimd.memset(causal[:], 1.0))
            for half in range(2):
                rows = slice(L * half, L * half + L)
                nc.gpsimd.affine_select(out=causal[rows], in_=causal[rows], compare_op=ALU.is_ge, fill=0.0, base=0,
                                        pattern=[[0, QUADS], [1, L]], channel_multiplier=-1).then_inc(masks, 1)
                pool.wait_ge(masks, 2 + half)
            for n in range(2):
                nc.gpsimd.memset(v_m[n][:], 0.0).then_inc(masks, 1)
            for n in range(2):
                nc.gpsimd.memset(k_q[n][:], 0.0).then_inc(masks, 1)
            for n in range(2):
                nc.gpsimd.memset(k_n[n][:], 0.0).then_inc(masks, 1)
            for n in range(2):
                chain.link(nc.gpsimd.memset(row_buf[n][:, :, 2 * C:ROW], 0.0))
                meta = row_buf[n][:].rearrange("p (b s) r -> p b s r", b=B)
                chain.link(nc.gpsimd.iota(meta[:, :, :, 2 * C], pattern=[[T, B], [P, 2]],
                                          base=-NO_TOKEN - n * 2 * P, channel_multiplier=1,
                                          allow_small_or_imprecise_dtypes=True))
                chain.link(nc.gpsimd.iota(meta[:, :, :, 2 * C + 1], pattern=[[1, B], [0, 2]], base=0,
                                          channel_multiplier=0, allow_small_or_imprecise_dtypes=True))
            nc.gpsimd.iota(iota_tok[:], pattern=[[0, E], [P, NT]], base=0, channel_multiplier=0,
                           allow_small_or_imprecise_dtypes=True).then_inc(masks, 1)
            nc.gpsimd.iota(iota_tile[:], pattern=[[1, ROUNDS * RING], [0, E]], base=0, channel_multiplier=0,
                           allow_small_or_imprecise_dtypes=True).then_inc(masks, 1)
            nc.gpsimd.iota(prefer[:], pattern=[[0, GT], [-1, E]], base=E, channel_multiplier=0,
                           allow_small_or_imprecise_dtypes=True).then_inc(masks, 1)
            nc.gpsimd.iota(counts[:], pattern=[[REGION, E], [0, GT + 1]], base=0, channel_multiplier=0,
                           allow_small_or_imprecise_dtypes=True).then_inc(masks, 1)
            nc.gpsimd.iota(region[:], pattern=[[REGION, E]], base=0, channel_multiplier=0,
                           allow_small_or_imprecise_dtypes=True).then_inc(masks, 1)
            chain.link(nc.gpsimd.memset(minus_half[:], -0.5))
            chain.link(nc.gpsimd.memset(carry[:], 1.0))
            nc.gpsimd.memset(carry[:, :, 0:1], 0.0).then_inc(masks, 1)

            gates = Count(pool, gate_chain)
            pool.wait_ge(var_ready, 2)
            nc.gpsimd.tensor_tensor(root[:, TAIL], var[:, TAIL], minus_half[:, 0:1].broadcast_to([P, NT - 2 * GT]), ALU.pow
                                    ).then_inc(root_ready, 1)
            pool.wait_ge(probs_ready, 2)
            for b in range(B):
                g_in = mod_bc[:, b, 0:4:3, :]
                gates.link(nc.gpsimd.tensor_scalar(gate_s[:, b], g_in, 0.0, None, ALU.is_ge))
                gates.link(nc.gpsimd.tensor_scalar(gate_s[:, b], gate_s[:, b], 2.0, -1.0, ALU.mult, ALU.add))
                gates.link(nc.gpsimd.tensor_tensor(gate_a[:, b], gate_s[:, b], g_in, ALU.mult))
                gates.link(nc.gpsimd.tensor_scalar(gate_a[:, b], gate_a[:, b], MOD_MIN, None, ALU.max))
                gates.link(nc.gpsimd.tensor_tensor(g_in, gate_a[:, b], gate_s[:, b], ALU.mult))
            pool.wait_ge(wproj_in, 16)
            for b in range(B):
                last = nc.gpsimd.tensor_tensor(wproj_b[:, b], wproj[:], mod_bc[:, b, 0], ALU.mult)
            gates.link(last)
            nc.gpsimd.tensor_scalar(mod_bc[:, :, 2, :], mod_bc[:, :, 2, :], 1.0, None, ALU.add
                                    ).then_inc(gates_ready, 1)

            def route_root(r):
                pool.wait_ge(var2_ready, r + 1)
                nc.gpsimd.tensor_tensor(guess2[:], var2[:], minus_half[:], ALU.pow).then_inc(guess2_ready, 1)

            def route_norm(r, par):
                ready = r + 1 if isinstance(r, int) else pool.to_reg(r + 1)
                x1, h2 = row_buf[par][:, :, C:2 * C], row_buf[par][:, :, 0:C]
                pool.wait_ge(masks, 2)
                pool.wait_ge(norm2_ready, ready)
                nc.gpsimd.tensor_tensor(h2, x1, mean2[:].unsqueeze(2).broadcast_to([P, GT, C]), ALU.subtract
                                        ).then_inc(centred, 1)
                pool.wait_ge(masks, 2)
                pool.wait_ge(centred, ready)
                nc.gpsimd.tensor_tensor(h2, h2, rstd2[:].unsqueeze(2).broadcast_to([P, GT, C]), ALU.mult
                                        ).then_inc(plain_ready, 1)

            def route_scatter(r, par):
                there = r + 1 if isinstance(r, int) else pool.to_reg(r + 1)
                pool.wait_ge(masks, 12)
                pool.wait_ge(slots_ready, there)
                for t in range(GT):
                    pool.indirect_dma_start(sorted_rows,
                                            bass.IndirectOffsetOnAxis(ap=slot_i[par][:, t:t + 1], axis=0),
                                            row_buf[par][:, t, :], None).then_inc(scattered[par], 16)

            def route(r, par, norm=True):
                route_root(r)
                if norm:
                    route_norm(r, par)
                route_scatter(r, par)

            with pool.Fori(0, G // 2 - 1) as k:
                route(2 * k, 0)
                route(2 * k + 1, 1)
            route(G - 2, 0)
            route(G - 1, 1, norm=False)

            def rows_out(n, ring):
                ready = n + 1 if isinstance(n, int) else pool.to_reg(n + 1)
                pool.wait_ge(scattered[0], 16 * NT // 2)
                pool.wait_ge(yrow_ready, ready)
                pool.indirect_dma_start(out_rows, bass.IndirectOffsetOnAxis(ap=slot_token[ring][:], axis=0),
                                        y_row[ring], None, bounds_check=B * T - 1, oob_is_err=False
                                        ).then_inc(row_out[ring], 16)

            with pool.Fori(0, ROUNDS - 1) as k:
                for ring in range(RING):
                    rows_out(RING * k + ring, ring)
            for n in range(RING * (ROUNDS - 1), SLOT_TILES):
                rows_out(n, n % RING)

        @blk.scalar
        def _(act):
            act.dma_start(wqkv[:], w_attn).then_inc(wqkv_in, 16)
            act.dma_start(wproj[:], w_proj).then_inc(wproj_in, 16)
            act.dma_start(wg_sb[:], wg).then_inc(wgate_in, 16)
            act.dma_start(bg_row[:], bg.rearrange("(o e) -> o e", o=1)).then_inc(wgate_in, 16)
            chain = Count(act, act_chain)
            act.wait_ge(c_in, 16)
            nc.scalar.activation(c_exp[:], c_col[:], ACT.Exp, scale=-1.0).then_inc(c_exp_done, 1)

            def front_norm(f):
                if not isinstance(f, int) or f:
                    if isinstance(f, int) and f == 2:
                        act.wait_ge(norm_ready, 2)
                    act.wait_ge(xt_mm, f)
                for t in range(GT):
                    n = GT * f + t
                    last = nc.scalar.activation(xhat[:, t:t + 1, :], x_all[:, bass.ds(n, 1), :], ACT.Identity,
                                                bias=shift[:, bass.ds(n, 1)], scale=rstd[:, bass.ds(n, 1)])
                last.then_inc(xhat_ready, 1)

            def front_ht(f):
                act.wait_ge(xt_mm, f + 1)
                for b in range(B):
                    cols = slice(2 * P * b, 2 * P * b + 2 * P)
                    last = nc.scalar.activation(h_t[:, cols], F0[:, cols], ACT.Identity, bias=sa_col[:, b:b + 1],
                                                scale=ca1_col[:, b:b + 1])
                last.then_inc(ht_ready, 1)

            def front_exp(f, chain):
                act.wait_ge(q_mm, f + 1)
                chain.link(nc.scalar.activation(relu_q[:], F1[:], ACT.Relu, scale=-1.0))
                act.wait_ge(q_ready, f)
                nc.scalar.activation(exp_q[:], relu_q[:], ACT.Exp, scale=-1.0).then_inc(eq_ready, 1)
                act.wait_ge(k_mm, f + 1)
                chain.link(nc.scalar.activation(relu_k[:], F2[:], ACT.Relu, scale=-1.0))
                act.wait_ge(k_ready, f)
                nc.scalar.activation(exp_k[:], relu_k[:], ACT.Exp, scale=-1.0).then_inc(ek_ready, 1)

            def masked_q(f, par):
                act.wait_ge(q_ready, f + 1)
                for a in range(QUADS):
                    last = nc.scalar.activation(q_m[par][:, a, :], q_t[par][:], ACT.Copy, scale=quad_head[:, a:a + 1])
                last.then_inc(qm_ready, 1)

            def front_v(f, par):
                act.wait_ge(v_mm, f + 1)
                nc.scalar.activation(v_n[par][:], F0[:].rearrange("p (n c) -> p n c", n=CHUNKS), ACT.Copy)
                for half in range(2):
                    rows = slice(L * half, L * half + L)
                    for a in range(2):
                        at = HD * (2 * half + a)
                        last = nc.scalar.activation(
                            v_m[par][rows, :, a, :].rearrange("p n (q r) -> p n q r", q=QUADS)[:, :, :, at:at + HD],
                            F0[rows].rearrange("p (n q a j) -> p n q a j", n=CHUNKS, q=QUADS, a=2)[:, :, :, a, :],
                            ACT.Copy)
                last.then_inc(v_ready, 1)
                act.wait_ge(k_ready, f + 1)
                for q in range(QUADS):
                    rows = slice(32 * q, 32 * q + 32)
                    last = nc.scalar.activation(k_q[par][rows, q, :], k_t[par][rows, :], ACT.Copy)
                last.then_inc(kq_ready, 1)

            def front_kn(f, par):
                act.wait_ge(kt_mm, f + 1)
                for half in range(2):
                    rows = slice(L * half, L * half + L)
                    last = nc.scalar.activation(
                        k_n[par][rows].rearrange("p n (q h r) -> p n q h r", q=QUADS, h=2)[:, :, :, half, :],
                        F1[rows].rearrange("p (n q r) -> p n q r", n=CHUNKS, q=QUADS), ACT.Copy)
                last.then_inc(kn_ready, 1)

            def front_rden(f, par):
                act.wait_ge(inv_mm, f + 1)
                nc.scalar.activation(rden[par][:], F2[:], ACT.Copy).then_inc(rden_ready, 1)

            def route_turned(r):
                act.wait_ge(h2t_mm, r + 1)
                nc.scalar.activation(h2_t[:], F0[:], ACT.Copy).then_inc(h2t_ready, 1)

            def step(g, par, chain, front=True, norm=True, route=True):
                f, fpar = g + 1, 1 - par
                if front:
                    front_ht(f)
                    front_exp(f, chain)
                    front_v(f, fpar)
                    front_kn(f, fpar)
                if norm:
                    front_norm(f + 1)
                if route:
                    route_turned(g - 1)
                if front:
                    masked_q(f, fpar)
                    front_rden(f, fpar)

            act.wait_ge(var_ready, 1)
            nc.scalar.activation(root[:, HEAD], var[:, HEAD], ACT.Sqrt).then_inc(root_ready, 1)
            act.wait_ge(norm_ready, 1)
            front_norm(0)
            front_ht(0)
            act.wait_ge(quad_ready, 1)
            front_exp(0, chain)
            act.wait_ge(masks, 9)
            masked_q(0, 0)
            front_v(0, 0)
            front_norm(1)
            front_kn(0, 0)
            front_rden(0, 0)
            step(0, 0, chain, route=False)
            before = chain.n
            with act.Fori(0, G // 2 - 2) as k:
                step(2 * k + 1, 1, Count(act, act_chain, before + 4 * k))
                step(2 * k + 2, 0, Count(act, act_chain, before + 4 * k + 2))
            chain.n = before + 2 * (G - 4)
            step(G - 3, 1, chain)
            step(G - 2, 0, chain, norm=False)
            step(G - 1, 1, None, front=False, norm=False)
            route_turned(G - 1)
            close_runs(act, range(1, E, 2))
            act.wait_ge(logit_mm, G)
            nc.scalar.activation(h2_t[:, 0:1], c_col[:, 0:1], ACT.Gelu_apprx_tanh)

            def column(n, par):
                wait_ge(act, up_mm, n - 1)
                act.wait_ge(row_mm, n + 1)
                nc.scalar.activation(h_col[par], [F0, F1][par][:, 0:P], ACT.Copy).then_inc(col_ready, 1)

            def hidden(n, par):
                wait_ge(act, down_mm, n - 1)
                act.wait_ge(up_mm, n + 1)
                nc.scalar.activation(gelu[par], [S0, S1][par][:].rearrange("p (k c) -> p k c", k=HC),
                                     ACT.Gelu_apprx_tanh).then_inc(gelu_ready, 1)

            def experts(k, edge):
                for j in range(RING):
                    n = RING * k + j
                    if edge < 1 or n < SLOT_TILES:
                        hidden(n, j % 2)
                    if edge < 1 or n + 2 < SLOT_TILES:
                        column(n + 2, j % 2)

            column(0, 0)
            column(1, 1)
            experts(0, 0)
            with act.Fori(1, ROUNDS - 1) as k:
                experts(k, 0)
            experts(ROUNDS - 1, 1)

        @blk.vector
        def _(dve):
            V = nc.vector
            chain = Count(dve, dve_chain)

            def spread(st, mean, diff, var, chain):
                V.tensor_tensor(diff, st[:, :, 1], st[:, :, 4], ALU.subtract)
                V.tensor_tensor(mean, st[:, :, 1], st[:, :, 4], ALU.add)
                chain.link(V.tensor_tensor(var, st[:, :, 2], st[:, :, 5], ALU.add))
                V.tensor_scalar(mean, mean, 0.5, None, ALU.mult)
                V.tensor_scalar(var, var, 1.0 / C, EPS, ALU.mult, ALU.add)
                chain.link(V.tensor_tensor(diff, diff, diff, ALU.mult))
                return V.scalar_tensor_tensor(out=var, in0=diff, scalar=0.25, in1=var, op0=ALU.mult, op1=ALU.add)

            def newton(rstd, guess, tmp, var, chain):
                chain.link(V.tensor_tensor(tmp, guess, guess, ALU.mult))
                chain.link(V.tensor_tensor(tmp, tmp, var, ALU.mult))
                chain.link(V.tensor_scalar(tmp, tmp, -0.5, 1.5, ALU.mult, ALU.add))
                return V.tensor_tensor(rstd, guess, tmp, ALU.mult)

            def first_spread(groups, tiles):
                for g in groups:
                    dve.wait_ge(x_in[g], 32)
                    for t in range(GT):
                        last = V.bn_stats(stats[:, GT * g + t, :], x_all[:, GT * g + t, :])
                chain.link(last)
                spread(stats[:, tiles, :], mean[:, tiles], diff[:, tiles], var[:, tiles], chain
                       ).then_inc(var_ready, 1)

            def first_rstd(tiles):
                chain.link(newton(rstd[:, tiles], root[:, tiles], diff[:, tiles], var[:, tiles], chain))
                V.scalar_tensor_tensor(out=shift[:, tiles], in0=mean[:, tiles], scalar=-1.0, in1=rstd[:, tiles],
                                       op0=ALU.mult, op1=ALU.mult).then_inc(norm_ready, 1)

            dve.wait_ge(c_exp_done, 1)
            chain.link(V.tensor_scalar(c_exp[:], c_exp[:], 1.0, None, ALU.add))
            chain.link(V.reciprocal(c_exp[:], c_exp[:]))
            chain.link(V.tensor_tensor(c_silu[:], c_col[:], c_exp[:], ALU.mult))
            dve.wait_ge(consts, 2)
            for b in range(B):
                last = V.tensor_scalar(c_bc[:, b, :], ones[:], c_silu[:, b:b + 1], None, ALU.mult)
            last.then_inc(c_ready, 1)
            first_spread(range(2), HEAD)
            dve.wait_ge(cols_mm, 1)
            V.tensor_copy(sa_col[:], F1[:, 0:B])
            V.tensor_scalar(ca1_col[:], F1[:, B:2 * B], 1.0, None, ALU.add)
            V.tensor_copy(bg_bc[:], F2[:, 0:E])
            dve.wait_ge(root_ready, 1)
            chain.link(V.reciprocal(root[:, HEAD], root[:, HEAD]))
            first_rstd(HEAD)
            dve.wait_ge(masks, 1)
            V.tensor_copy(block_b[:], block[:].unsqueeze(1).broadcast_to([P, B, P]))
            V.tensor_reduce(quad_head[:], block[:].rearrange("p (q a j) -> p a q j", q=QUADS, a=QUADS)[:, :, :, 0],
                            AX.X, ALU.add).then_inc(quad_ready, 1)
            V.memset(den[:, 0:1], 0.0).then_inc(y_ready, 2)
            V.memset(den[:, 1:2], 0.0).then_inc(x1_ready, 1)
            first_spread(range(2, G), TAIL)
            dve.wait_ge(mod_mm, 1)
            for b in range(B):
                last = V.tensor_copy(mod_bc[:, b].rearrange("p k c -> p (k c)"), [S0, S1][b][:])
                last.then_inc(probs_ready, 1)
            dve.wait_ge(masks, 3)

            def front_elu_q(f, par):
                dve.wait_ge(eq_ready, f + 1)
                V.scalar_tensor_tensor(out=q_t[par][:], in0=F1[:], scalar=0.0, in1=exp_q[:], op0=ALU.max,
                                       op1=ALU.add).then_inc(q_ready, 1)

            def front_elu_k(f, par):
                dve.wait_ge(ek_ready, f + 1)
                V.scalar_tensor_tensor(out=k_t[par][:], in0=F2[:], scalar=0.0, in1=exp_k[:], op0=ALU.max,
                                       op1=ALU.add).then_inc(k_ready, 1)

            def first_z_and_rden(chain):
                dve.wait_ge(k_ready, 1)
                for b in range(B):
                    cols = slice(2 * P * b, 2 * P * b + 2 * P)
                    last = V.tensor_tensor_scan(z_t[0][:, cols], ones[:, 0:1].broadcast_to([P, 2 * P]),
                                                k_t[0][:, cols], 0.0, ALU.mult, ALU.add)
                chain.link(last)
                V.tensor_tensor(qz[:], z_t[0][:], q_t[0][:], ALU.mult).then_inc(qz_ready, 1)
                rden_and_slots(0, 0, 0, chain, True, False)

            def core_probs(g, s, b, quads=range(QUADS)):
                wait_ge(dve, y_mm, 4 * g + 2 * s - 1)
                for q in quads:
                    dve.wait_ge(score_mm, 16 * g + 8 * s + 4 * b + q + 1)
                    V.tensor_tensor(probs[:, s, b, q, :], score_bank[q % 2][:, 0:QUADS * L],
                                    causal[:].rearrange("p a t -> p (a t)"), ALU.mult).then_inc(probs_ready, 1)

            def core_state(g, u):
                dve.wait_ge(kv_mm, 4 * g + u + 1)
                V.tensor_tensor(state[:, u % 2].rearrange("p b (q h r) -> p (b q) h r", q=QUADS, h=2),
                                ST[:, 0:B * L].rearrange("p (n r) -> p n r", r=2 * HD).unsqueeze(2).broadcast_to(
                                    [P, B * QUADS, 2, 2 * HD]),
                                block_b[:].rearrange("p b (q h r) -> p (b q) h r", q=QUADS, h=2), ALU.mult
                                ).then_inc(state_ready, 1)

            def core_y(g, par, u):
                s, half = u // 2, u % 2
                if u == 0:
                    dve.wait_ge(rden_ready, g + 1)
                dve.wait_ge(y_mm, 4 * g + u + 2)
                r = rden[par][:].rearrange("p (b s h t) -> p b s h t", b=B, s=2, h=2)[:, :, s, half, :]
                V.tensor_tensor(y_n[:, s, :, L * half:L * half + L],
                                y_bank[half][:, 0:2 * L].rearrange("p (b t) -> p b t", b=B), r,
                                ALU.mult).then_inc(y_ready, 1)

            def core_x1(g, par, turn):
                if par:
                    dve.wait_ge(scattered[1], 16 * GT * turn + 16)
                elif not isinstance(g, int) or g:
                    dve.wait_ge(scattered[0], 16 * GT * turn)
                if not isinstance(g, int) or g:
                    V.tensor_scalar(row_buf[par][:, :, 2 * C], row_buf[par][:, :, 2 * C], 4.0 * P, None, ALU.add)
                dve.wait_ge(proj_mm, g + 1)
                V.tensor_tensor(row_buf[par][:, :, C:2 * C], x_all[:, bass.ds(GT * g, GT), :],
                                F0[:].rearrange("p (t c) -> p t c", t=GT), ALU.add).then_inc(x1_ready, 1)

            def route_stats(r, par, chain):
                dve.wait_ge(x1_ready, r + 2)
                for t in range(GT):
                    last = V.bn_stats(stats2[:, t, :], row_buf[par][:, t, C:2 * C])
                if not isinstance(r, int) or r:
                    dve.wait_ge(plain_ready, r)
                chain.link(last)
                spread(stats2[:], mean2[:], diff2[:], var2[:], chain).then_inc(var2_ready, 1)

            def route_newton(r, chain):
                dve.wait_ge(guess2_ready, r + 1)
                newton(rstd2[:], guess2[:], newton2[:], var2[:], chain).then_inc(norm2_ready, 1)

            def route_modulate(r, par, chain, norm=False):
                if norm:
                    for t in range(GT):
                        last = V.tensor_scalar(row_buf[par][:, t, 0:C], row_buf[par][:, t, C:2 * C],
                                               mean2[:, t:t + 1], rstd2[:, t:t + 1], ALU.subtract, ALU.mult)
                    chain.link(last)
                else:
                    dve.wait_ge(plain_ready, r + 1)
                h2 = row_buf[par][:, :, 0:C].rearrange("p (b s) c -> p b s c", b=B)
                chain.link(V.tensor_tensor(h2, h2, mod_bc[:, :, 2, :].unsqueeze(2).broadcast_to([P, B, 2, C]),
                                           ALU.mult))
                V.tensor_tensor(h2, h2, mod_bc[:, :, 1, :].unsqueeze(2).broadcast_to([P, B, 2, C]),
                                ALU.add).then_inc(h2_ready, 1)

            def z_and_argmax(f, par, r, chain, front, route):
                def scan(b):
                    return V.tensor_tensor_scan(z_t[par][:, 2 * P * b:2 * P * b + 2 * P],
                                                ones[:, 0:1].broadcast_to([P, 2 * P]),
                                                k_t[par][:, 2 * P * b:2 * P * b + 2 * P],
                                                z_t[1 - par][:, 2 * P * b + 2 * P - 1:2 * P * b + 2 * P],
                                                ALU.mult, ALU.add)

                if route:
                    dve.wait_ge(logit_mm, r + 1)
                    a = V.tensor_tensor(logit[:], LOGIT.rearrange("p (n e) -> p n e", e=E),
                                        bg_bc[:].unsqueeze(1).broadcast_to([P, GT, E]), ALU.add)
                if front:
                    dve.wait_ge(k_ready, f + 1)
                chain.link(a if route else None, scan(0) if front else None)
                if route:
                    a = V.tensor_reduce(best[:], logit[:], AX.X, ALU.max)
                chain.link(a if route else None, scan(1) if front else None)
                if route:
                    a = V.tensor_tensor(logit[:], logit[:], best[:].unsqueeze(2).broadcast_to([P, GT, E]), ALU.is_ge)
                if front:
                    V.tensor_tensor(qz[:], z_t[par][:], q_t[par][:], ALU.mult).then_inc(qz_ready, 1)
                if route:
                    chain.link(a)
                    chain.link(V.tensor_tensor(logit[:], logit[:], prefer[:], ALU.mult))
                    chain.link(V.tensor_reduce(best[:], logit[:], AX.X, ALU.max))
                    V.tensor_tensor(onehot[:], logit[:], best[:].unsqueeze(2).broadcast_to([P, GT, E]),
                                    ALU.is_equal).then_inc(onehot_ready, 1)

            def rden_and_slots(f, r, par, chain, front, route):
                if front:
                    dve.wait_ge(den_mm, f + 1)
                    b = V.tensor_scalar(den[:], F2[:, 0:GT * HEADS], DEN_EPS, None, ALU.add)
                if route:
                    dve.wait_ge(rank_mm, r + 1)
                    a = V.tensor_copy(counts[:, :, 1:GT + 1], TOTAL.rearrange("p (n e) -> p e n", e=E))
                chain.link(a if route else None, b if front else None)
                if front:
                    b = V.reciprocal(den_inv[:], den[:])
                if route:
                    a = V.tensor_tensor_scan(place[:].rearrange("p e n -> p (e n)"),
                                             carry[:].rearrange("p e n -> p (e n)"),
                                             counts[:].rearrange("p e n -> p (e n)"), 0.0, ALU.mult, ALU.add)
                chain.link(a if route else None, b if front else None)
                if route:
                    a = V.tensor_tensor(pick_row[:], RANK.rearrange("p (n e) -> p n e", e=E),
                                        place[:, :, 0:GT].rearrange("p e n -> p n e"), ALU.add)
                if front:
                    V.tensor_copy(qz[:].rearrange("p (n j) -> p n j", j=HD),
                                  den_inv[:].unsqueeze(2).broadcast_to([P, GT * HEADS, HD])).then_inc(inv_ready, 1)
                if route:
                    chain.link(a)
                    a = V.tensor_tensor(pick_row[:], pick_row[:], onehot[:], ALU.mult)
                    V.tensor_copy(counts[:, :, 0:1], place[:, :, GT:GT + 1])
                    chain.link(a)
                    chain.link(V.tensor_reduce(slot_f[:], pick_row[:], AX.X, ALU.add))
                    V.tensor_copy(slot_i[par][:], slot_f[:]).then_inc(slots_ready, 1)

            LINKS = 3 + 3 + 1 + 7 + 7

            def step(g, par, turn, chain, front=True, route=True):
                f, fpar = g + 1, 1 - par
                n = chain.n
                core_probs(g, 0, 1, LAST)
                if route:
                    route_stats(g - 1, 1 - par, chain)
                core_y(g, par, 0)
                if route:
                    route_newton(g - 1, chain)
                if front:
                    front_elu_q(f, fpar)
                    front_elu_k(f, fpar)
                core_state(g, 2)
                core_probs(g, 1, 0, FIRST)
                core_probs(g, 1, 0, LAST)
                core_y(g, par, 1)
                if route:
                    route_modulate(g - 1, 1 - par, chain)
                core_probs(g, 1, 1, FIRST)
                core_probs(g, 1, 1, LAST)
                core_state(g, 3)
                z_and_argmax(f, fpar, g - 1, chain, front, route)
                core_y(g, par, 2)
                if front:
                    core_state(g, 4)
                    core_probs(f, 0, 0, FIRST)
                rden_and_slots(f, g - 1, 1 - par, chain, front, route)
                if front:
                    core_probs(f, 0, 0, LAST)
                core_y(g, par, 3)
                if front:
                    core_state(f, 1)
                    core_probs(f, 0, 1, FIRST)
                core_x1(g, par, turn)
                if front and route:
                    assert chain.n - n == LINKS, chain.n - n

            front_elu_q(0, 0)
            front_elu_k(0, 0)
            first_z_and_rden(chain)
            core_state(0, 0)
            core_probs(0, 0, 0)
            core_state(0, 1)
            core_probs(0, 0, 1, FIRST)
            dve.wait_ge(root_ready, 2)
            first_rstd(TAIL)
            step(0, 0, 0, chain, route=False)
            dve.wait_ge(masks, 15)
            dve.wait_ge(gates_ready, 1)
            V.tensor_tensor(gb_diff[:], mod_bc[:, 1, 3], mod_bc[:, 0, 3], ALU.subtract)
            before = chain.n
            with dve.Fori(0, G // 2 - 1) as k:
                step(2 * k + 1, 1, k, Count(dve, dve_chain, before + 2 * LINKS * k))
                step(2 * k + 2, 0, k + 1, Count(dve, dve_chain, before + 2 * LINKS * k + LINKS))
            chain.n = before + LINKS * (G - 2)
            step(G - 1, 1, G // 2 - 1, chain, front=False)
            route_stats(G - 1, 1, chain)
            route_newton(G - 1, chain)
            dve.wait_ge(norm2_ready, G)
            route_modulate(G - 1, 1, chain, norm=True)
            z_and_argmax(G, 0, G - 1, chain, False, True)
            rden_and_slots(G, G - 1, 1, chain, False, True)

            V.tensor_copy(tail_i[:], place[0:1, :, GT]).then_inc(tails_ready, 1)
            chain.link(V.tensor_tensor(cnt[:], place[0:1, :, GT], region[:], ALU.subtract))
            chain.link(V.tensor_tensor(r_cmp[:], cnt[:].unsqueeze(2).broadcast_to([1, E, NT]), iota_tok[:], ALU.is_gt))
            chain.link(V.tensor_reduce(tiles_e[:], r_cmp[:], AX.X, ALU.add))
            chain.link(V.tensor_tensor_scan(tiles_cum[:], ones[0:1, 0:1].broadcast_to([1, E]), tiles_e[:], 0.0,
                                            ALU.mult, ALU.add))
            V.tensor_scalar(tiles_e[:], tiles_e[:], -1.0, float(EXPERT_TILES), ALU.mult, ALU.add)
            chain.link(V.tensor_tensor(t_cmp[:], tiles_cum[:].unsqueeze(1).broadcast_to([1, ROUNDS * RING, E]),
                                       iota_tile[:], ALU.is_le))
            V.tensor_reduce(t_exp[:], t_cmp[:], AX.X, ALU.add)
            chain.link(V.tensor_tensor(t_skip[:], t_cmp[:], tiles_e[:].unsqueeze(1).broadcast_to(
                [1, ROUNDS * RING, E]), ALU.mult))
            V.tensor_scalar(t_exp[:], t_exp[:], float(E - 1), None, ALU.min)
            chain.link(V.tensor_reduce(t_row[:], t_skip[:], AX.X, ALU.add))
            chain.link(V.tensor_tensor(t_row[:], t_row[:], iota_tile[:, :, 0], ALU.add))
            chain.link(V.tensor_scalar(t_row[:], t_row[:], float(E * EXPERT_TILES), None, ALU.min))
            V.tensor_copy(t_row_i[:], t_row[:]).then_inc(table_ready, 1)
            t_ring = t_exp[:].rearrange("o (n r) -> o n r", r=RING)
            chain.link(V.scalar_tensor_tensor(out=code[:], in0=t_ring[:, :, RING - 1], scalar=float(E),
                                              in1=t_ring[:, :, RING - 2],
                                              op0=ALU.mult, op1=ALU.add))
            for j in range(RING - 3, -1, -1):
                chain.link(V.scalar_tensor_tensor(out=code[:], in0=code[:], scalar=float(E), in1=t_ring[:, :, j],
                                                  op0=ALU.mult, op1=ALU.add))
            chain.link(V.tensor_copy(t_code[:], code[:]))

            dve.wait_ge(w1_in, 16)
            dve.wait_ge(w2_in, 16)

            def pick_w1(n, wbuf, code, j):
                wait_ge(dve, up_mm, n - WBUFS + 1)
                V.tensor_copy(w1_cur[wbuf], w1_all[:, bass.ds((code >> (3 * j)) & (E - 1), 1)].rearrange(
                    "p o h -> p (o h)")).then_inc(w1c_ready, 1)

            def pick_w2(n, wbuf, code, j):
                wait_ge(dve, down_mm, n - WBUFS + 1)
                V.tensor_copy(w2_cur[wbuf], w2_all[:, bass.ds((code >> (3 * j)) & (E - 1), 1)].rearrange(
                    "p o k c -> p (o k) c")).then_inc(w2c_ready, 1)

            def finish(n, par, ring, k):
                row = slot_row[ring]
                wait_ge(dve, row_in[ring], 16 * k + 16)
                V.scalar_tensor_tensor(out=gb_sel[par], in0=gb_diff[:], scalar=row[:, 2 * C + 1:2 * C + 2],
                                       in1=mod_bc[:, 0, 3], op0=ALU.mult, op1=ALU.add).then_inc(gated_ready, 1)
                wait_ge(dve, row_out[ring], 16 * k)
                V.tensor_scalar(slot_token[ring][:], row[:, 2 * C:2 * C + 1], float(NO_TOKEN), None, ALU.add)
                dve.wait_ge(down_mm, n + 1)
                dve.wait_ge(gated_ready, 2 * n + 1)
                V.tensor_tensor(y_gated[par], [Y0, Y1][par][:, 0:C], gb_sel[par], ALU.mult
                                ).then_inc(gated_ready, 1)
                dve.wait_ge(gated_ready, 2 * n + 2)
                V.tensor_tensor(y_row[ring], y_gated[par], row[:, C:2 * C], ALU.add).then_inc(yrow_ready, 1)

            def experts(k, edge):
                code = dve.value_load(t_code[0:1, bass.ds(k, 1)] if not isinstance(k, int) else t_code[0:1, k:k + 1],
                                      min_val=0, max_val=E ** RING - 1)
                for j in range(RING):
                    n = RING * k + j
                    there = not edge or n < SLOT_TILES
                    if there:
                        pick_w1(n, j % WBUFS, code, j)
                        pick_w2(n, j % WBUFS, code, j)
                    if not isinstance(n, int) or 3 <= n < SLOT_TILES + 3:
                        finish(n - 3, (j + 1) % 2, (j - 3) % RING, k if j >= 3 else k - 1)

            experts(0, False)
            with dve.Fori(1, ROUNDS - 1) as k:
                experts(k, False)
            experts(ROUNDS - 1, True)
            for n in range(RING * ROUNDS - 3, SLOT_TILES):
                finish(n, n % 2, n % RING, ROUNDS - 1)

        @blk.tensor
        def _(pe):
            mm = nc.tensor.matmul
            pe.wait_ge(c_ready, 1)
            pe.wait_ge(wmod_in, 16)
            pe.wait_ge(wgate_in, 32)
            pe.wait_ge(consts, 2)
            for k in range(2):
                mm(F1[:, B * k:B * k + B], wmod_sb[:, k * C:(k + 1) * C], c_silu[:], start=True, stop=True)
            mm(F2[:, 0:E], ones[0:1, :], bg_row[:], start=True, stop=True).then_inc(cols_mm, 1)
            for b in range(B):
                mm([S0, S1][b][:], c_bc[:, b, :], wmod_sb[:, 2 * C:6 * C], start=True, stop=True)
            pe.wait_ge(pool_chain, 1)
            mm(ST[:, 0:P], zeros[:, 0:P], zeros[:, 0:P], start=True, stop=True).then_inc(kv_mm, 1)
            mm(ST[:, 0:P], zeros[:, 0:P], zeros[:, 0:P], start=False, stop=True,
               skip_group_check=True).then_inc(y_mm, 1)
            mm(ST[:, 0:P], zeros[:, 0:P], zeros[:, 0:P], start=False, stop=True,
               skip_group_check=True).then_inc(mod_mm, 1)

            def front_x(f):
                pe.wait_ge(xhat_ready, f + 1)
                pe.wait_ge(v_ready, f)
                if not isinstance(f, int) or f >= 1:
                    pe.wait_ge(x1_ready, f)
                for t in range(GT):
                    last = nc.tensor.transpose(F0[:, t * P:(t + 1) * P], xhat[:, t, :], ident[:])
                last.then_inc(xt_mm, 1)

            def front_qkv(f):
                pe.wait_ge(ht_ready, f + 1)
                pe.wait_ge(kn_ready, f)
                mm(F1[:], wqkv[:, 0:C], h_t[:], start=True, stop=True).then_inc(q_mm, 1)
                pe.wait_ge(rden_ready, f)
                mm(F2[:], wqkv[:, C:2 * C], h_t[:], start=True, stop=True).then_inc(k_mm, 1)
                wv = wqkv[:, 2 * C:3 * C].rearrange("p (q h r) -> p q h r", q=QUADS, h=2)
                for n in range(CHUNKS):
                    for half in range(2):
                        last = mm(F0[L * half:L * half + L, n * L:(n + 1) * L], h_t[:, n * L:(n + 1) * L],
                                  wv[:, :, half, :], start=True, stop=True)
                last.then_inc(v_mm, 1)

            def front_kt(f, par):
                pe.wait_ge(k_ready, f + 1)
                eye = ident[:].rearrange("p (q h r) -> p q h r", q=QUADS, h=2)
                for n in range(CHUNKS):
                    for half in range(2):
                        last = mm(F1[L * half:L * half + L, n * L:(n + 1) * L], k_t[par][:, n * L:(n + 1) * L],
                                  eye[:, :, half, :], start=True, stop=True)
                last.then_inc(kt_mm, 1)

            def front_den(f):
                pe.wait_ge(qz_ready, f + 1)
                for t in range(GT):
                    last = mm(F2[:, HEADS * t:HEADS * t + HEADS], qz[:, t * P:(t + 1) * P],
                              block[:].rearrange("p (h j) -> p h j", j=HD)[:, :, 0], start=True, stop=True)
                last.then_inc(den_mm, 1)

            def front_inv(f):
                pe.wait_ge(inv_ready, f + 1)
                for t in range(GT):
                    last = nc.tensor.transpose(F2[:, t * P:(t + 1) * P], qz[:, t * P:(t + 1) * P], ident[:])
                last.then_inc(inv_mm, 1)

            def core_scores(g, par, s, b, quads=range(QUADS)):
                t = 2 * b + s
                if s == 0 and b == 0:
                    pe.wait_ge(qm_ready, g + 1)
                    pe.wait_ge(kq_ready, g + 1)
                for q in quads:
                    pe.wait_ge(probs_ready, 16 * g + 8 * s + 4 * b + q + 1)
                    for n in range(2):
                        tok = t * P + n * L
                        for half in range(2):
                            last = mm(score_bank[q % 2][L * half:L * half + L, 2 * L * n:2 * L * n + 2 * L],
                                      k_q[par][:, q, tok:tok + L], q_m[par][:, 2 * half:2 * half + 2, tok:tok + L],
                                      start=True, stop=True)
                    last.then_inc(score_mm, 1)

            def core_across(g, par, u):
                s, half = u // 2, u % 2
                pe.wait_ge(state_ready, 4 * g + u + 1)
                pe.wait_ge(y_ready, 4 * g + u + 1)
                for b in range(B):
                    tok = (2 * b + s) * P + half * L
                    mm(y_bank[half][:, b * L:b * L + L], state[:, half, b, :], q_t[par][:, tok:tok + L],
                       start=(b == 0), stop=False, skip_group_check=True)
                if u == 0:
                    pe.wait_ge(kn_ready, g + 1)
                    pe.wait_ge(v_ready, g + 1)
                for b in range(B):
                    n = 2 * (2 * b + s) + half
                    last = mm(ST[:, b * L:(b + 1) * L], k_n[par][:, n, :], v_n[par][:, n, :], start=False,
                              stop=True, skip_group_check=True)
                last.then_inc(kv_mm, 1)

            def core_within(g, par, u):
                s, half = u // 2, u % 2
                masked = 2 + 16 * g + 8 * s + 8
                masked = masked if isinstance(masked, int) else pe.to_reg(masked)
                pe.wait_ge(masks, 5)
                pe.wait_ge(probs_ready, masked)
                for b in range(B):
                    for a in range(2):
                        for q in range(QUADS):
                            last = mm(y_bank[half][32 * q:32 * q + 32, b * L:b * L + L],
                                      v_m[par][:, 2 * (2 * b + s) + half, a, 32 * q:32 * q + 32],
                                      probs[:, s, b, q, (2 * half + a) * L:(2 * half + a + 1) * L], start=False,
                                      stop=(a == 1), skip_group_check=True)
                last.then_inc(y_mm, 1)

            def core_proj(g, front, route):
                if route:
                    pe.wait_ge(slots_ready, g)
                elif front:
                    pe.wait_ge(v_ready, g + 2)
                pe.wait_ge(y_ready, 2 + 4 * g + 4)
                for t in range(GT):
                    last = mm(F0[:, t * P:(t + 1) * P], y_n[:, t % 2, t // 2, :], wproj_b[:, t // 2, :],
                              start=True, stop=True)
                last.then_inc(proj_mm, 1)

            def route_turn(r, par, front=False):
                pe.wait_ge(h2_ready, r + 1)
                if front:
                    pe.wait_ge(v_ready, r + 3)
                for t in range(GT):
                    last = nc.tensor.transpose(F0[:, t * P:(t + 1) * P], row_buf[par][:, t, 0:C], ident[:])
                last.then_inc(h2t_mm, 1)

            def route_logits(r):
                pe.wait_ge(h2t_ready, r + 1)
                for t in range(GT):
                    last = mm(LOGIT[:, t * E:(t + 1) * E], h2_t[:, t * P:(t + 1) * P], wg_sb[:],
                              start=True, stop=True)
                last.then_inc(logit_mm, 1)

            def route_rank(r):
                pe.wait_ge(onehot_ready, r + 1)
                hot = onehot[:].rearrange("p n e -> p (n e)")
                mm(RANK, upper[:], hot, start=True, stop=True)
                mm(TOTAL, ones[:], hot, start=True, stop=True).then_inc(rank_mm, 1)

            def step(g, par, front=True, route=True):
                f, fpar = g + 1, 1 - par
                core_scores(g, par, 0, 1, LAST)
                if front:
                    front_x(f)
                core_within(g, par, 0)
                if front:
                    front_qkv(f)
                core_across(g, par, 1)
                core_scores(g, par, 1, 0, FIRST)
                core_scores(g, par, 1, 0, LAST)
                core_within(g, par, 1)
                if front:
                    front_kt(f, fpar)
                core_across(g, par, 2)
                core_scores(g, par, 1, 1, FIRST)
                if route:
                    route_turn(g - 1, 1 - par, front)
                core_scores(g, par, 1, 1, LAST)
                if route:
                    route_logits(g - 1)
                core_within(g, par, 2)
                core_across(g, par, 3)
                if front:
                    core_scores(f, fpar, 0, 0, FIRST)
                    front_den(f)
                if route:
                    route_rank(g - 1)
                core_within(g, par, 3)
                if front:
                    core_scores(f, fpar, 0, 0, LAST)
                    core_across(f, fpar, 0)
                    core_scores(f, fpar, 0, 1, FIRST)
                    front_inv(f)
                core_proj(g, front, route)

            front_x(0)
            pe.wait_ge(wqkv_in, 16)
            front_qkv(0)
            front_kt(0, 0)
            front_den(0)
            front_inv(0)
            core_scores(0, 0, 0, 0)
            core_across(0, 0, 0)
            core_scores(0, 0, 0, 1, FIRST)
            pe.wait_ge(gates_ready, 1)
            step(0, 0, route=False)
            with pe.Fori(0, G // 2 - 1) as k:
                step(2 * k + 1, 1)
                step(2 * k + 2, 0)
            step(G - 1, 1, front=False)
            route_turn(G - 1, 1)
            route_logits(G - 1)
            route_rank(G - 1)
            pe.wait_ge(slots_ready, G)

            def expert_turn(n, ring, k):
                pe.wait_ge(row_in[ring], 16 * k + 16)
                wait_ge(pe, col_ready, n - 1)
                nc.tensor.transpose([F0, F1][ring % 2][:, 0:P], slot_row[ring][:, 0:C], ident[:]).then_inc(row_mm, 1)

            def expert_up(n, par, wbuf):
                pe.wait_ge(w1c_ready, n + 1)
                pe.wait_ge(col_ready, n + 1)
                wait_ge(pe, gelu_ready, n - 1)
                for j in range(HC):
                    last = mm([S0, S1][par][:, j * P:(j + 1) * P], w1_cur[wbuf][:, j * P:(j + 1) * P], h_col[par],
                              start=True, stop=True)
                last.then_inc(up_mm, 1)

            def expert_down(n, par, wbuf):
                pe.wait_ge(gelu_ready, n + 1)
                pe.wait_ge(w2c_ready, n + 1)
                wait_ge(pe, gated_ready, 2 * n - 2)
                for j in range(HC):
                    last = mm([Y0, Y1][par][:, 0:C], gelu[par][:, j, :], w2_cur[wbuf][:, j, :], start=(j == 0),
                              stop=(j == HC - 1))
                last.then_inc(down_mm, 1)

            def experts(k, edge):
                for j in range(RING):
                    n = RING * k + j
                    if not edge or n + 2 < SLOT_TILES:
                        expert_turn(n + 2, (j + 2) % RING, k + (j + 2) // RING)
                    if not edge or n + 1 < SLOT_TILES:
                        expert_up(n + 1, (j + 1) % 2, (j + 1) % WBUFS)
                    if not edge or n < SLOT_TILES:
                        expert_down(n, j % 2, j % WBUFS)

            expert_turn(0, 0, 0)
            expert_turn(1, 1, 0)
            expert_up(0, 0, 0)
            experts(0, False)
            with pe.Fori(1, ROUNDS - 1) as k:
                experts(k, False)
            experts(ROUNDS - 1, True)


_INS = ['L0_attn_x', 'L0_attn_w_attn', 'L0_attn_w_proj', 'L0_ffn_W1', 'L0_ffn_W2', 'L0_ffn_Wg', 'L0_ffn_bg', 'L0_c',
        'L0_wmod']
_OUTS = [((2, 2048, 128), 'float32')]


def kernel(**inputs):
    import numpy as _np
    import concourse.bacc as _bacc
    from concourse import mybir as _mybir
    from concourse.bass_utils import run_bass_kernel_spmd as _run

    nc = _bacc.Bacc("TRN2", target_bir_lowering=False, num_devices=1)
    arrays, args = {}, []
    for name in _INS:
        a = _np.ascontiguousarray(inputs[name])
        arrays[f"in_{name}_dram"] = a
        args.append(nc.dram_tensor(f"in_{name}_dram", a.shape, _mybir.dt.from_np(a.dtype), kind="ExternalInput").ap())
    for i, (shape, dtype) in enumerate(_OUTS):
        dt = _mybir.dt.from_np(_np.dtype(dtype))
        args.append(nc.dram_tensor(f"out_{i}_dram", shape, dt, kind="ExternalOutput").ap())
    build(nc, *args)
    r = _run(nc, [arrays], core_ids=[0])
    got = tuple(r.results[0][f"out_{i}_dram"] for i in range(len(_OUTS)))
    return got[0]
```
